# Optimizing a Trainium2 kernel written in Bass

```python
import numpy as np
import jax
import jax.numpy as jnp

def _softmax(x, axis=-1):
    return jax.nn.softmax(x, axis=axis)

def _gelu(x):
    return jax.nn.gelu(x, approximate=True)

def _silu(x):
    return jax.nn.silu(x)

def _sigmoid(x):
    return jax.nn.sigmoid(x)

def _layernorm(x, axis=-1, eps=1e-05):
    m = jnp.mean(x, axis=axis, keepdims=True)
    v = jnp.var(x, axis=axis, keepdims=True)
    return (x - m) / jnp.sqrt(v + eps)

def _scatter_add(tgt, idx, src, axis=0):
    return tgt.at[idx].add(src)

def _segment_sum(src, seg, n):
    return jax.ops.segment_sum(src, seg, n)
kernel_name = 'mk_adj_preln_d4_adj_r2_a557b7'

def setup_inputs(seed: int=0):
    np.random.seed(seed)
    _w = jnp.asarray

    def _rec_inputs():
        import jax
        import jax.numpy as jnp
        _gk = jax.random.key(seed)
        x = -0.0001538 + 1 * jax.random.normal(jax.random.fold_in(_gk, 1), (64, 128, 384), jnp.float32)
        _a = jax.random.bernoulli(jax.random.fold_in(_gk, 2), 0.125, (64, 128, 128))
        _a = jnp.logical_or(_a, jnp.swapaxes(_a, -1, -2))
        _a = jnp.logical_or(_a, jnp.eye(128, dtype=bool))
        _af = _a.astype(jnp.float32)
        _af = _af * jax.random.uniform(jax.random.fold_in(_gk, 3), (64, 128, 128), jnp.float32, 0.05, 0.999992)
        adj = _af
        return (x, adj)
    x, adj = _rec_inputs()

    def _L0_gnn_setup():
        import jax, jax.numpy as jnp
        import numpy as np
        B, N, D, H = (8, 512, 384, 12)
        HD = D // H

        def _split_heads(x):
            b, n, _ = x.shape
            return x.reshape(b, n, H, HD).transpose(0, 2, 1, 3)
        key = jax.random.key(seed)
        ks = jax.random.split(key, 10)
        input_graph = jax.random.normal(ks[0], (B, N, D), dtype=jnp.float32)
        u = jax.random.uniform(ks[1], (B, N, N), dtype=jnp.float32)
        keep = jax.random.uniform(ks[2], (B, N, N)) < 0.15
        adj = jnp.where(keep, u, 0.0)
        s = 1.0 / np.sqrt(D)
        Wq = jax.random.normal(ks[3], (D, D), dtype=jnp.float32) * s
        bq = jnp.zeros((D,), dtype=jnp.float32)
        Wk = jax.random.normal(ks[4], (D, D), dtype=jnp.float32) * s
        bk = jnp.zeros((D,), dtype=jnp.float32)
        Wv = jax.random.normal(ks[5], (D, D), dtype=jnp.float32) * s
        bv = jnp.zeros((D,), dtype=jnp.float32)
        beta = jnp.asarray(0.1, dtype=jnp.float32)
        return {'input_graph': input_graph, 'adj': adj, 'Wq': Wq, 'bq': bq, 'Wk': Wk, 'bk': bk, 'Wv': Wv, 'bv': bv, 'beta': beta}
    _L0_gnn_all = _L0_gnn_setup()
    _L0_gnn_in = {k: v for k, v in _L0_gnn_all.items() if k in ('Wq', 'bq', 'Wk', 'bk', 'Wv', 'bv', 'beta')}
    del _L0_gnn_all

    def _L1_gnn_setup():
        import jax, jax.numpy as jnp
        import numpy as np
        B, S, H, L = (32, 256, 384, 2)

        def _layer_norm(z, a, b, eps=0.001):
            mu = jnp.mean(z, axis=-1, keepdims=True)
            sigma = jnp.std(z, axis=-1, keepdims=True, ddof=1)
            return (z - mu) / (sigma + eps) * a + b
        key = jax.random.key(seed)
        ks = jax.random.split(key, 6)
        hidden_state = jax.random.normal(ks[0], (B, S, H), dtype=jnp.float32)
        adjacency_matrix = (jax.random.uniform(ks[1], (B, S, S)) < 0.2).astype(jnp.float32)
        W_left = 0.05 * jax.random.normal(ks[2], (L, H, H), dtype=jnp.float32)
        W_right = 0.05 * jax.random.normal(ks[3], (L, H, H), dtype=jnp.float32)
        W_lin = 0.05 * jax.random.normal(ks[4], (L, H, H), dtype=jnp.float32)
        b_lin = jnp.zeros((L, H), dtype=jnp.float32)
        ln_a = jnp.ones((L, H), dtype=jnp.float32)
        ln_b = jnp.zeros((L, H), dtype=jnp.float32)
        return {'hidden_state': hidden_state, 'adjacency_matrix': adjacency_matrix, 'W_left': W_left, 'W_right': W_right, 'W_lin': W_lin, 'b_lin': b_lin, 'ln_a': ln_a, 'ln_b': ln_b}
    _L1_gnn_all = _L1_gnn_setup()
    _L1_gnn_in = {k: v for k, v in _L1_gnn_all.items() if k in ('W_left', 'W_right', 'W_lin', 'b_lin', 'ln_a', 'ln_b')}
    del _L1_gnn_all

    def _L2_gnn_setup():
        import jax, jax.numpy as jnp
        import numpy as np
        LN_EPS = 1e-12

        def _digcn_forward(hidden_state, adjacency_matrix, Wl, bl, Ws, bs, Wr, br, ln_w, ln_b):
            B, S, D = hidden_state.shape
            temper = jnp.asarray(D, jnp.float32) ** 0.5
            i = jnp.arange(S)
            upper = (i[None, :] > i[:, None]).astype(hidden_state.dtype)
            lower = (i[None, :] < i[:, None]).astype(hidden_state.dtype)

            def layer(h, params):
                wl, b_l, ws, b_s, wr, b_r, g, beta = params
                u = jnp.einsum('bid,bjd->bij', h, h) / temper
                a = jax.nn.softmax(u, axis=-1)
                delta = a * adjacency_matrix
                attn = delta / (jnp.sum(delta, axis=-1, keepdims=True) + 1e-10)
                hl = h @ wl.T + b_l
                hs = h @ ws.T + b_s
                hr = h @ wr.T + b_r
                diag_a = jnp.diagonal(attn, axis1=1, axis2=2)
                ctx = jnp.einsum('bij,bjd->bid', attn * upper, hl) + diag_a[..., None] * hs + jnp.einsum('bij,bjd->bid', attn * lower, hr)
                mean = ctx.mean(-1, keepdims=True)
                var = ctx.var(-1, keepdims=True)
                o = (ctx - mean) / jnp.sqrt(var + LN_EPS) * g + beta
                return (jax.nn.relu(o), None)
            out, _ = jax.lax.scan(layer, hidden_state, (Wl, bl, Ws, bs, Wr, br, ln_w, ln_b))
            return out
        key = jax.random.key(seed)
        ks = jax.random.split(key, 6)
        B, S, D, L = (8, 512, 384, 2)
        scale = (1.0 / D) ** 0.5
        hidden_state = jax.random.normal(ks[0], (B, S, D), jnp.float32)
        adjacency_matrix = (jax.random.uniform(ks[1], (B, S, S)) < 0.05).astype(jnp.float32)
        Wl = jax.random.normal(ks[2], (L, D, D), jnp.float32) * scale
        Ws = jax.random.normal(ks[3], (L, D, D), jnp.float32) * scale
        Wr = jax.random.normal(ks[4], (L, D, D), jnp.float32) * scale
        bl = jnp.zeros((L, D), jnp.float32)
        bs = jnp.zeros((L, D), jnp.float32)
        br = jnp.zeros((L, D), jnp.float32)
        ln_w = jnp.ones((L, D), jnp.float32)
        ln_b = jnp.zeros((L, D), jnp.float32)
        return dict(hidden_state=hidden_state, adjacency_matrix=adjacency_matrix, Wl=Wl, bl=bl, Ws=Ws, bs=bs, Wr=Wr, br=br, ln_w=ln_w, ln_b=ln_b)
    _L2_gnn_all = _L2_gnn_setup()
    _L2_gnn_in = {k: v for k, v in _L2_gnn_all.items() if k in ('Wl', 'bl', 'Ws', 'bs', 'Wr', 'br', 'ln_w', 'ln_b')}
    del _L2_gnn_all

    def _L3_gnn_setup():
        import jax, jax.numpy as jnp
        import numpy as np
        NUM_HEADS = 12
        HIDDEN = 384
        HEAD = HIDDEN // NUM_HEADS
        SCALE = HIDDEN ** (-0.5)
        key = jax.random.key(seed)
        ks = jax.random.split(key, 8)
        B, N = (16, 256)
        std = HIDDEN ** (-0.5)
        return {'x': jax.random.normal(ks[0], (B, N, HIDDEN), dtype=jnp.float32), 'encoding_bias': jax.random.normal(ks[1], (B, N, N), dtype=jnp.float32), 'Wq': jax.random.normal(ks[2], (HIDDEN, HIDDEN), dtype=jnp.float32) * std, 'Wk': jax.random.normal(ks[3], (HIDDEN, HIDDEN), dtype=jnp.float32) * std, 'Wv': jax.random.normal(ks[4], (HIDDEN, HIDDEN), dtype=jnp.float32) * std, 'bv': jax.random.normal(ks[5], (HIDDEN,), dtype=jnp.float32) * 0.01, 'Wo': jax.random.normal(ks[6], (HIDDEN, HIDDEN), dtype=jnp.float32) * std, 'bo': jax.random.normal(ks[7], (HIDDEN,), dtype=jnp.float32) * 0.01}
    _L3_gnn_all = _L3_gnn_setup()
    _L3_gnn_in = {k: v for k, v in _L3_gnn_all.items() if k in ('Wq', 'Wk', 'Wv', 'bv', 'Wo', 'bo')}
    del _L3_gnn_all
    return {'x': x, 'adj': adj, 'L0_gnn_Wq': _L0_gnn_in['Wq'], 'L0_gnn_bq': _L0_gnn_in['bq'], 'L0_gnn_Wk': _L0_gnn_in['Wk'], 'L0_gnn_bk': _L0_gnn_in['bk'], 'L0_gnn_Wv': _L0_gnn_in['Wv'], 'L0_gnn_bv': _L0_gnn_in['bv'], 'L0_gnn_beta': _L0_gnn_in['beta'], 'L1_gnn_W_left': _L1_gnn_in['W_left'], 'L1_gnn_W_right': _L1_gnn_in['W_right'], 'L1_gnn_W_lin': _L1_gnn_in['W_lin'], 'L1_gnn_b_lin': _L1_gnn_in['b_lin'], 'L1_gnn_ln_a': _L1_gnn_in['ln_a'], 'L1_gnn_ln_b': _L1_gnn_in['ln_b'], 'L2_gnn_Wl': _L2_gnn_in['Wl'], 'L2_gnn_bl': _L2_gnn_in['bl'], 'L2_gnn_Ws': _L2_gnn_in['Ws'], 'L2_gnn_bs': _L2_gnn_in['bs'], 'L2_gnn_Wr': _L2_gnn_in['Wr'], 'L2_gnn_br': _L2_gnn_in['br'], 'L2_gnn_ln_w': _L2_gnn_in['ln_w'], 'L2_gnn_ln_b': _L2_gnn_in['ln_b'], 'L3_gnn_Wq': _L3_gnn_in['Wq'], 'L3_gnn_Wk': _L3_gnn_in['Wk'], 'L3_gnn_Wv': _L3_gnn_in['Wv'], 'L3_gnn_bv': _L3_gnn_in['bv'], 'L3_gnn_Wo': _L3_gnn_in['Wo'], 'L3_gnn_bo': _L3_gnn_in['bo']}

def reference(x, adj, L0_gnn_Wq, L0_gnn_bq, L0_gnn_Wk, L0_gnn_bk, L0_gnn_Wv, L0_gnn_bv, L0_gnn_beta, L1_gnn_W_left, L1_gnn_W_right, L1_gnn_W_lin, L1_gnn_b_lin, L1_gnn_ln_a, L1_gnn_ln_b, L2_gnn_Wl, L2_gnn_bl, L2_gnn_Ws, L2_gnn_bs, L2_gnn_Wr, L2_gnn_br, L2_gnn_ln_w, L2_gnn_ln_b, L3_gnn_Wq, L3_gnn_Wk, L3_gnn_Wv, L3_gnn_bv, L3_gnn_Wo, L3_gnn_bo):
    import jax
    import jax.numpy as jnp

    def _L0_gnn_ref(input_graph, adj, Wq, bq, Wk, bk, Wv, bv, beta):
        import jax, jax.numpy as jnp
        import numpy as np
        B, N, D, H = (8, 512, 384, 12)
        HD = D // H

        def _split_heads(x):
            b, n, _ = x.shape
            return x.reshape(b, n, H, HD).transpose(0, 2, 1, 3)
        q = _split_heads(input_graph @ Wq + bq)
        k = _split_heads(input_graph @ Wk + bk)
        v = _split_heads(input_graph @ Wv + bv)
        scores = jnp.einsum('bhqd,bhkd->bhqk', q, k) / jnp.sqrt(jnp.asarray(HD, input_graph.dtype))
        adj_e = adj[:, None, :, :]
        scores = scores + beta * adj_e
        scores = jnp.where(adj_e > 0, scores, jnp.asarray(-9000000000000000.0, scores.dtype))
        probs = jax.nn.softmax(scores, axis=-1)
        out = jnp.einsum('bhqk,bhkd->bhqd', probs, v)
        return out.transpose(0, 2, 1, 3).reshape(input_graph.shape[0], input_graph.shape[1], D)

    def _L1_gnn_ref(hidden_state, adjacency_matrix, W_left, W_right, W_lin, b_lin, ln_a, ln_b):
        import jax, jax.numpy as jnp
        import numpy as np
        B, S, H, L = (32, 256, 384, 2)

        def _layer_norm(z, a, b, eps=0.001):
            mu = jnp.mean(z, axis=-1, keepdims=True)
            sigma = jnp.std(z, axis=-1, keepdims=True, ddof=1)
            return (z - mu) / (sigma + eps) * a + b
        temper = float(np.sqrt(H))
        adj = adjacency_matrix
        adj_tri = jnp.triu(adj, k=1)
        diag_mask = jnp.triu(adj, k=0) - adj_tri
        h = hidden_state
        for l in range(L):
            m_left = jnp.einsum('bsh,oh->bso', h, W_left[l])
            m_right = jnp.einsum('bsh,oh->bso', h, W_right[l])
            u_left = jnp.einsum('bih,bjh->bij', h, m_left) / temper
            u_right = jnp.einsum('bih,bjh->bij', h, m_right) / temper
            u = u_left * adj_tri + u_left * diag_mask + u_right * jnp.swapaxes(adj_tri, 1, 2)
            delta_exp_u = jnp.exp(u) * adj
            attention = delta_exp_u / (jnp.sum(delta_exp_u, axis=2, keepdims=True) + 1e-10)
            h_lin = jnp.einsum('bsh,oh->bso', h, W_lin[l]) + b_lin[l]
            ctx = jnp.matmul(attention, h_lin)
            h = jax.nn.relu(_layer_norm(ctx, ln_a[l], ln_b[l]))
        return h

    def _L2_gnn_ref(hidden_state, adjacency_matrix, Wl, bl, Ws, bs, Wr, br, ln_w, ln_b):
        import jax, jax.numpy as jnp
        import numpy as np
        LN_EPS = 1e-12

        def _digcn_forward(hidden_state, adjacency_matrix, Wl, bl, Ws, bs, Wr, br, ln_w, ln_b):
            B, S, D = hidden_state.shape
            temper = jnp.asarray(D, jnp.float32) ** 0.5
            i = jnp.arange(S)
            upper = (i[None, :] > i[:, None]).astype(hidden_state.dtype)
            lower = (i[None, :] < i[:, None]).astype(hidden_state.dtype)

            def layer(h, params):
                wl, b_l, ws, b_s, wr, b_r, g, beta = params
                u = jnp.einsum('bid,bjd->bij', h, h) / temper
                a = jax.nn.softmax(u, axis=-1)
                delta = a * adjacency_matrix
                attn = delta / (jnp.sum(delta, axis=-1, keepdims=True) + 1e-10)
                hl = h @ wl.T + b_l
                hs = h @ ws.T + b_s
                hr = h @ wr.T + b_r
                diag_a = jnp.diagonal(attn, axis1=1, axis2=2)
                ctx = jnp.einsum('bij,bjd->bid', attn * upper, hl) + diag_a[..., None] * hs + jnp.einsum('bij,bjd->bid', attn * lower, hr)
                mean = ctx.mean(-1, keepdims=True)
                var = ctx.var(-1, keepdims=True)
                o = (ctx - mean) / jnp.sqrt(var + LN_EPS) * g + beta
                return (jax.nn.relu(o), None)
            out, _ = jax.lax.scan(layer, hidden_state, (Wl, bl, Ws, bs, Wr, br, ln_w, ln_b))
            return out
        return _digcn_forward(hidden_state, adjacency_matrix, Wl, bl, Ws, bs, Wr, br, ln_w, ln_b)

    def _L3_gnn_ref(x, encoding_bias, Wq, Wk, Wv, bv, Wo, bo):
        import jax, jax.numpy as jnp
        import numpy as np
        NUM_HEADS = 12
        HIDDEN = 384
        HEAD = HIDDEN // NUM_HEADS
        SCALE = HIDDEN ** (-0.5)
        B, N, _ = x.shape
        q = (x @ Wq.T).reshape(B, N, NUM_HEADS, HEAD)
        k = (x @ Wk.T).reshape(B, N, NUM_HEADS, HEAD)
        v = (x @ Wv.T + bv).reshape(B, N, NUM_HEADS, HEAD)
        a = jnp.einsum('bnhd,bmhd->bhnm', q, k) * SCALE + encoding_bias[:, None, :, :]
        pad_mask = jnp.all(a == 0, axis=-1)
        a = jnp.where(pad_mask[..., None], -jnp.inf, a)
        a = jax.nn.softmax(a, axis=-1)
        a = jnp.nan_to_num(a)
        o = jnp.einsum('bhnm,bmhd->bnhd', a, v).reshape(B, N, HIDDEN)
        return o @ Wo.T + bo
    h = jnp.maximum(_layernorm(x, axis=-1), 0.0)
    x = x + _L0_gnn_ref(h, adj, L0_gnn_Wq, L0_gnn_bq, L0_gnn_Wk, L0_gnn_bk, L0_gnn_Wv, L0_gnn_bv, L0_gnn_beta)
    h = jnp.maximum(_layernorm(x, axis=-1), 0.0)
    x = x + _L1_gnn_ref(h, adj, L1_gnn_W_left, L1_gnn_W_right, L1_gnn_W_lin, L1_gnn_b_lin, L1_gnn_ln_a, L1_gnn_ln_b)
    h = jnp.maximum(_layernorm(x, axis=-1), 0.0)
    x = x + _L2_gnn_ref(h, adj, L2_gnn_Wl, L2_gnn_bl, L2_gnn_Ws, L2_gnn_bs, L2_gnn_Wr, L2_gnn_br, L2_gnn_ln_w, L2_gnn_ln_b)
    h = jnp.maximum(_layernorm(x, axis=-1), 0.0)
    x = x + _L3_gnn_ref(h, adj, L3_gnn_Wq, L3_gnn_Wk, L3_gnn_Wv, L3_gnn_bv, L3_gnn_Wo, L3_gnn_bo)
    return x

_drawn_inputs = setup_inputs


def setup_inputs(seed=0):
    import zlib

    import numpy as np

    out = dict(_drawn_inputs(seed))
    spreads = {'L0_gnn_bq': (0.0, 0.8),
     'L0_gnn_bk': (0.0, 0.8),
     'L0_gnn_bv': (0.0, 0.1),
     'L1_gnn_b_lin': (0.0, 0.1),
     'L1_gnn_ln_a': (1.0, 0.2),
     'L1_gnn_ln_b': (0.0, 0.1),
     'L2_gnn_bl': (0.0, 0.1),
     'L2_gnn_bs': (0.0, 0.1),
     'L2_gnn_br': (0.0, 0.1),
     'L2_gnn_ln_w': (1.0, 0.2),
     'L2_gnn_ln_b': (0.0, 0.1)}
    factors = {'L1_gnn_W_left': 7.42,
     'L1_gnn_W_right': 8.0,
     'L3_gnn_Wq': 8.0,
     'L3_gnn_Wk': 8.0,
     'L3_gnn_bv': 8.0,
     'L3_gnn_bo': 8.0}
    for name, (base, spread) in spreads.items():
        noise = np.random.default_rng([zlib.crc32(name.encode()), seed]).standard_normal(out[name].shape)
        drawn = base * np.exp(spread * noise) if base else spread * noise
        out[name] = jnp.asarray(drawn.astype(out[name].dtype))
    for name, factor in factors.items():
        out[name] = (out[name] * factor).astype(out[name].dtype)
    return out
```

```python
from contextlib import ExitStack

import concourse.bass as bass
from concourse import mybir

ALU = mybir.AluOpType
ACT = mybir.ActivationFunctionType
AX_X = mybir.AxisListType.X
F32 = mybir.dt.float32
F16 = mybir.dt.float16

P = 128
D = 384
C = D // P
G = 2
STREAMS = 2
TOK = G * P
H = 12
HD = D // H
HPC = P // HD
BANKS = 8
WS = 16.0

GAT, DIR_A, DIR_B, DIG_A, DIG_B, GRAPHORMER = range(6)
ATTENTION = (GAT, GRAPHORMER)
W0 = {GAT: 0, DIR_A: 3, DIR_B: 6, DIG_A: 9, DIG_B: 12, GRAPHORMER: 15}
N_W = 19
ROW_V = {GAT: [0], DIR_A: [1], DIR_B: [2], DIG_A: [3, 4, 5], DIG_B: [6, 7, 8], GRAPHORMER: [9]}
ROW_BO = 10
ROW_LN = {DIR_A: 11, DIR_B: 13, DIG_A: 15, DIG_B: 17}
N_ROWS = 19
MASKED = -9000000000000000.0
PAD_SHIFT = 1.0e5


def stream_steps(s):
    out = []

    def add(name, layer=None, i=None):
        out.append((s, name, layer, i))

    add("load")
    for layer in range(6):
        if layer not in (DIR_B, DIG_B):
            add("stats", layer)
            add("norm", layer)
        for g in range(G):
            add("turn", layer, g)
        if layer in ATTENTION or layer in (DIR_A, DIR_B):
            for m in range(C):
                add("proj", layer, m)
        if layer in ATTENTION:
            for g in range(G):
                add("vals", layer, g)
            for g in range(G):
                add("scores", layer, g)
            for g in range(G):
                for c in range(C):
                    add("flip", layer, (g, c))
                add("mix", layer, g)
                if layer == GAT:
                    add("back", layer, g)
                else:
                    add("project", layer, g)
        else:
            add("gram", layer)
            for j in range(len(ROW_V[layer])):
                for g in range(G):
                    add("vals", layer, j * G + g)
                if j == 0:
                    add("soft", layer)
            add("aturn", layer)
            for g in range(G):
                add("context", layer, g)
            add("cnorm", layer)
            if layer in (DIR_B, DIG_B):
                add("residual", layer)
    add("finish")
    return out


LAG = 14


def schedule():
    a, b = stream_steps(0), stream_steps(1)
    out = []
    for i in range(len(a) + LAG):
        if i < len(a):
            out.append(a[i])
        if i >= LAG:
            out.append(b[i - LAG])
    return out


def banks_of(name):
    return {"load": 1, "turn": 1, "proj": 1, "vals": 1, "scores": HPC, "flip": 1, "mix": 2, "back": 1, "project": 1,
            "gram": 1, "aturn": 1, "context": 1}.get(name, 0)


def signals_of(step):
    s, name, layer, i = step
    if name == "load":
        return ["sides"]
    if name == "stats":
        return ["var", "rstd"]
    if name == "norm":
        return ["shift"] + ["normed"] * G
    if name == "turn":
        return ["turn_hi", "turn_lo"]
    if name == "proj":
        return ["proj_hi", "proj_lo"]
    if name == "vals":
        return ["vals"]
    if name == "scores":
        return ["scored"] * HPC + ["logits", "centred"]
    if name == "flip":
        return ["probs"]
    if name == "mix":
        return ["mixed"] + (["mixed_hi", "mixed_lo"] if layer == GRAPHORMER else [])
    if name == "back":
        return ["x_added"]
    if name == "project":
        return ["y"]
    if name == "gram":
        return ["gram", "gram_exp"]
    if name == "soft":
        return ["soft"]
    if name == "aturn":
        return ["aturn_dir" if layer in (DIR_A, DIR_B) else "aturn_dig"]
    if name == "cnorm":
        return ["cvar", "crstd", "cshift"] + ["cnormed"] * G + ["affine"]
    if name == "residual":
        return ["x_added"]
    if name == "finish":
        return ["y_biased"]
    return []


RELEASE = {"load": "sides", "turn": "turn_lo", "proj": "proj_lo", "vals": "vals", "scores": "scored", "flip": "probs", "mix": "mixed",
           "back": "x_added", "project": "y", "gram": "gram", "context": "cnormed"}


def release_of(step, j):
    s, name, layer, i = step
    if name == "aturn":
        return "aturn_dir" if layer in (DIR_A, DIR_B) else "aturn_dig", step, 0
    if name == "context":
        return "cnormed", (s, "cnorm", layer, None), i
    return RELEASE[name], step, j if name == "scores" else 0


class Plan:

    def __init__(self):
        self.steps = schedule()
        self.total, self.nth = {}, {}
        self.fills = 0
        self.bank = {}
        self.user = {}
        last = {}
        for step in self.steps:
            for n, sig in enumerate(signals_of(step)):
                self.nth.setdefault((sig, step), []).append(self.total.get(sig, 0))
                self.total[sig] = self.total.get(sig, 0) + 1
            self.bank[step] = []
            for j in range(banks_of(step[1])):
                b = self.fills % BANKS
                self.bank[step].append((b, self.fills))
                self.user[step, j] = (last.get(b), False)
                last[b] = (step, j)
                self.fills += 1
        for key, (before, _) in self.user.items():
            if before is None:
                self.user[key] = (last[self.bank[key[0]][key[1]][0]], True)


SIGNALS = {
    "sides": "vector",
    "var": "vector", "shift": "vector", "turn_lo": "vector", "proj_lo": "vector", "vals": "vector", "scored": "vector",
    "logits": "vector", "mixed": "vector", "mixed_lo": "vector", "x_added": "vector", "y": "vector", "gram": "vector",
    "soft": "vector", "aturn_dig": "vector", "cvar": "vector", "cshift": "vector",
    "normed": "scalar", "turn_hi": "scalar", "proj_hi": "scalar", "probs": "scalar", "mixed_hi": "scalar",
    "gram_exp": "scalar", "aturn_dir": "scalar", "cnormed": "scalar",
    "rstd": "pool", "centred": "pool", "crstd": "pool", "affine": "pool", "y_biased": "pool",
}
VECTOR_HANDOVERS = 110


def graph_layers_kernel(nc, x, adj, weights, rows, qk_bias, beta, out):
    N = x.shape[0]
    ROUNDS = N // (G * STREAMS)
    plan = Plan()
    steps = plan.steps

    with ExitStack() as ctx:
        def sb(name, shape, dt=F32):
            return ctx.enter_context(nc.sbuf_tensor(name, shape, dt))

        def sem(name):
            return ctx.enter_context(nc.semaphore(name))

        w_hi = sb("w_hi", [P, N_W, C, D], F16)
        w_lo = sb("w_lo", [P, N_W, C, D], F16)
        row = sb("row", [P, N_ROWS, D])
        bias_qk = sb("bias_qk", [P, 2, C])
        beta_col = sb("beta_col", [P, 1])
        ident = sb("ident", [P, P])
        tri_dir = sb("tri_dir", [P, 2, P])
        tri_dig = sb("tri_dig", [P, 3, P])
        ones = sb("ones", [P, HD])
        powers = sb("powers", [P, 2, G])
        pad_col = sb("pad_col", [P, 1])

        X = [sb(f"x{s}", [P, G, D]) for s in range(STREAMS)]
        A = [sb(f"adj{s}", [P, G, P]) for s in range(STREAMS)]
        HN = [sb(f"h{s}", [P, G, D]) for s in range(STREAMS)]
        HT = [sb(f"ht{s}", [P, 2, C, TOK], F16) for s in range(STREAMS)]
        QK = [sb(f"qk{s}", [P, 2, C, 2, TOK], F16) for s in range(STREAMS)]
        V = [sb(f"v{s}", [P, G, D]) for s in range(STREAMS)]
        T = [sb(f"t{s}", [P, G, H, P]) for s in range(STREAMS)]
        PT = [sb(f"pt{s}", [P, H, P]) for s in range(STREAMS)]
        RD = [sb(f"rd{s}", [P, C, P]) for s in range(STREAMS)]
        OT = [sb(f"ot{s}", [P, C, P]) for s in range(STREAMS)]
        OHL = [sb(f"ohl{s}", [P, 2, C, P], F16) for s in range(STREAMS)]
        B0 = [sb(f"b0_{s}", [P, G, P]) for s in range(STREAMS)]
        AA = [sb(f"aa{s}", [P, G, 2, P]) for s in range(STREAMS)]
        ST = [sb(f"st{s}", [P, G, 6]) for s in range(STREAMS)]
        MV = [sb(f"mv{s}", [P, G, 2]) for s in range(STREAMS)]
        VE = [sb(f"ve{s}", [P, G]) for s in range(STREAMS)]
        RS = [sb(f"rs{s}", [P, G]) for s in range(STREAMS)]
        RI = [sb(f"ri{s}", [P, G]) for s in range(STREAMS)]
        SH = [sb(f"sh{s}", [P, G]) for s in range(STREAMS)]
        MX = [sb(f"mx{s}", [P, G, H]) for s in range(STREAMS)]
        AM = [sb(f"am{s}", [P, G, H]) for s in range(STREAMS)]
        SE = [sb(f"se{s}", [P, G]) for s in range(STREAMS)]
        SD = [sb(f"sd{s}", [P, G]) for s in range(STREAMS)]
        SR = [sb(f"sr{s}", [P, G]) for s in range(STREAMS)]

        flat = [T[s][:].rearrange("p g h k -> p (g h k)") for s in range(STREAMS)]
        V1 = [f[:, 0:768].rearrange("p (g d) -> p g d", g=G) for f in flat]
        V2 = [f[:, 768:1536].rearrange("p (g d) -> p g d", g=G) for f in flat]
        U2 = [f[:, 0:512].rearrange("p (g w k) -> p g w k", g=G, w=2) for f in flat]
        UW = [f[:, 512:768].rearrange("p (g k) -> p g k", g=G) for f in flat]
        UW2 = [f[:, 1536:1792].rearrange("p (g k) -> p g k", g=G) for f in flat]
        E = [f[:, 1792:2048].rearrange("p (g k) -> p g k", g=G) for f in flat]
        DL = [f[:, 2048:2304].rearrange("p (g k) -> p g k", g=G) for f in flat]
        AT = [f[:, 2304:3072].rearrange("p (w g k) -> p w g k", w=3, g=G) for f in flat]

        bank = [ctx.enter_context(nc.psum_tensor(f"bank{b}", [P, 512], F32)) for b in range(BANKS)]

        done = {name: sem(name) for name in SIGNALS}
        filled = sem("bank_filled")
        x_in = [sem(f"x_in{s}") for s in range(STREAMS)]
        x_free = [sem(f"x_free{s}") for s in range(STREAMS)]
        prep = [sem(f"adj_prepared{s}") for s in range(STREAMS)]
        stored = [sem(f"stored{s}") for s in range(STREAMS)]
        w_in = [sem(f"w_in{i}") for i in range(4)]
        w_hi_done, w_lo_done = sem("w_hi_done"), sem("w_lo_done")
        vector_setup = sem("vector_setup")
        rows_in, consts_done, setup_done = sem("rows_in"), sem("consts_done"), sem("setup_done")
        vector_step, pool_step, pool_setup = sem("vector_step"), sem("pool_step"), sem("pool_setup")

        x_v = x.rearrange("(n g) p d -> n p g d", g=G)
        adj_v = adj.rearrange("(n g) p k -> n p g k", g=G)
        out_v = out.rearrange("(n g) p d -> n p g d", g=G)
        w_v = weights.rearrange("w (c p) n -> w p c n", p=P)

        def wait_for(eng, it, sig, step, n=0):
            eng.wait_ge(done[sig], it * plan.total[sig] + (plan.total[sig] + plan.nth[sig, step][n] + 1))

        def wait_filled(eng, it, step, j=0):
            eng.wait_ge(filled, it * plan.fills + (plan.bank[step][j][1] + 1))

        def wait_emptied(eng, it, step, j=0):
            (before, k), a_round_ago = plan.user[step, j]
            sig, giver, n = release_of(before, k)
            eng.wait_ge(done[sig], it * plan.total[sig] + ((not a_round_ago) * plan.total[sig] + plan.nth[sig, giver][n] + 1))

        def start_ahead(eng, engine):
            for sig, giver in SIGNALS.items():
                if giver == engine:
                    eng.sem_inc(done[sig], plan.total[sig])

        def bank_of(step, j=0):
            return bank[plan.bank[step][j][0]]

        stage = [flat[i // 2][:, (i % 2) * 1536:(i % 2) * 1536 + C * D].rearrange("p (c n) -> p c n", c=C)
                 for i in range(4)]
        block = ctx.enter_context(nc.Block())

        @block.sync
        def _(sp):
            sp.dma_start(row[:], rows.rearrange("(a r) d -> a r d", a=1).broadcast_to((P, N_ROWS, D))).then_inc(rows_in, 16)
            sp.dma_start(bias_qk[:], qk_bias).then_inc(rows_in, 16)
            sp.dma_start(beta_col[:], beta.rearrange("(a b) -> a b", a=1).broadcast_to((P, 1))).then_inc(rows_in, 16)
            for w in range(N_W):
                if w >= 4:
                    sp.wait_ge(w_lo_done, w - 3)
                sp.dma_start(stage[w % 4], w_v[w]).then_inc(w_in[w % 4], 16)
            with sp.Fori(0, ROUNDS) as it:
                for step in steps:
                    s, name, layer, i = step
                    if name == "load":
                        sp.wait_ge(x_free[s], it + 1)
                        n = it * STREAMS + s
                        sp.dma_start(X[s][:], x_v[bass.ds(n, 1)].rearrange("a p g d -> (a p) g d")).then_inc(x_in[s], 16)
                        sp.dma_start(A[s][:], adj_v[bass.ds(n, 1)].rearrange("a p g d -> (a p) g d")).then_inc(x_in[s], 16)

        @block.gpsimd
        def _(pool):
            n = 0

            def select(view, op, base, pattern, cm):
                nonlocal n
                nc.gpsimd.memset(view, 1.0).then_inc(pool_setup, 1)
                n += 1
                pool.wait_ge(pool_setup, n)
                return nc.gpsimd.affine_select(out=view, in_=view, compare_op=op, fill=0.0, base=base,
                                               pattern=[[pattern, P]], channel_multiplier=cm)

            select(ident[:], ALU.is_equal, 0, -1, 1)
            select(tri_dir[:, 0, :], ALU.is_ge, 0, 1, -1)
            select(tri_dir[:, 1, :], ALU.is_ge, -1, -1, 1)
            select(tri_dig[:, 0, :], ALU.is_ge, -1, -1, 1)
            select(tri_dig[:, 1, :], ALU.is_equal, 0, -1, 1)
            select(tri_dig[:, 2, :], ALU.is_ge, -1, 1, -1)
            nc.gpsimd.memset(powers[:, 0, :], -0.5)
            nc.gpsimd.memset(powers[:, 1, :], 0.5)
            nc.gpsimd.memset(ones[:], 1.0).then_inc(consts_done, 1)
            pool.wait_ge(consts_done, 1)
            pool.wait_ge(rows_in, 48)
            start_ahead(pool, "pool")
            steps_done = 0
            per_round = 4 * STREAMS
            with pool.Fori(0, ROUNDS) as it:
                for step in steps:
                    s, name, layer, i = step
                    if name == "stats":
                        wait_for(pool, it, "var", step)
                        nc.gpsimd.tensor_tensor(RS[s][:], VE[s][:], powers[:, 0, :], ALU.pow).then_inc(done["rstd"], 1)
                    elif name == "scores":
                        wait_for(pool, it, "logits", step)
                        nc.gpsimd.tensor_tensor(T[s][:, i], T[s][:, i],
                                                MX[s][:, i, :].unsqueeze(2).broadcast_to((P, H, P)),
                                                ALU.subtract).then_inc(done["centred"], 1)
                    elif name == "cnorm":
                        wait_for(pool, it, "cvar", step)
                        which = 1 if layer in (DIR_A, DIR_B) else 0
                        nc.gpsimd.tensor_tensor(RS[s][:], VE[s][:], powers[:, which, :], ALU.pow).then_inc(done["crstd"], 1)
                        wait_for(pool, it, "cnormed", step, G - 1)
                        r = ROW_LN[layer]
                        nc.gpsimd.tensor_tensor(HN[s][:], HN[s][:], row[:, r, :].unsqueeze(1).broadcast_to((P, G, D)),
                                                ALU.mult).then_inc(pool_step, 1)
                        steps_done += 1
                        pool.wait_ge(pool_step, it * per_round + steps_done)
                        nc.gpsimd.tensor_tensor(HN[s][:], HN[s][:],
                                                row[:, r + 1, :].unsqueeze(1).broadcast_to((P, G, D)),
                                                ALU.add).then_inc(done["affine"], 1)
                    elif name == "finish":
                        last = (s, "project", GRAPHORMER, G - 1)
                        wait_for(pool, it, "y", last)
                        nc.gpsimd.tensor_tensor(HN[s][:], HN[s][:],
                                                row[:, ROW_BO, :].unsqueeze(1).broadcast_to((P, G, D)),
                                                ALU.add).then_inc(done["y_biased"], 1)
                assert steps_done == per_round

        @block.scalar
        def _(act):
            for w in range(N_W):
                act.wait_ge(w_in[w % 4], 16 * (w // 4 + 1))
                nc.scalar.activation(w_hi[:, w], stage[w % 4], ACT.Copy, scale=WS).then_inc(w_hi_done, 1)
            start_ahead(act, "scalar")
            act.wait_ge(setup_done, 1)
            with act.Fori(0, ROUNDS) as it:
                for step in steps:
                    s, name, layer, i = step
                    if name == "norm":
                        wait_for(act, it, "shift", step)
                        if layer == GAT:
                            act.wait_ge(stored[s], it * 16 + 16)
                        for g in range(G):
                            nc.scalar.activation(HN[s][:, g], X[s][:, g], ACT.Identity, bias=SH[s][:, g:g + 1],
                                                 scale=RS[s][:, g:g + 1]).then_inc(done["normed"], 1)
                    elif name == "turn":
                        wait_filled(act, it, step)
                        nc.scalar.activation(HT[s][:, 0, :, i * P:(i + 1) * P],
                                             bank_of(step)[:, 0:D].rearrange("p (c k) -> p c k", c=C),
                                             ACT.Relu).then_inc(done["turn_hi"], 1)
                    elif name == "proj":
                        wait_filled(act, it, step)
                        if layer == GAT:
                            for side in range(2):
                                last = nc.scalar.activation(QK[s][:, 0, i, side], bank_of(step)[:, side * TOK:(side + 1) * TOK],
                                                            ACT.Identity, bias=bias_qk[:, side, i:i + 1])
                        else:
                            last = nc.scalar.activation(QK[s][:, 0, i].rearrange("p a t -> p (a t)"), bank_of(step)[:, :], ACT.Copy)
                        last.then_inc(done["proj_hi"], 1)
                    elif name == "flip":
                        g, c = i
                        wait_filled(act, it, step)
                        nc.scalar.activation(PT[s][:, HPC * c:HPC * (c + 1)].rearrange("p h k -> p (h k)"),
                                             bank_of(step)[:, :], ACT.Exp).then_inc(done["probs"], 1)
                    elif name == "mix" and layer == GRAPHORMER:
                        wait_for(act, it, "mixed", step)
                        nc.scalar.activation(OHL[s][:, 0], OT[s][:], ACT.Copy).then_inc(done["mixed_hi"], 1)
                    elif name == "gram":
                        wait_for(act, it, "gram", step)
                        src = UW[s] if layer in (DIR_A, DIR_B) else UW2[s]
                        scale = 1.0 / (WS * D ** 0.5) if layer in (DIR_A, DIR_B) else 1.0 / D ** 0.5
                        nc.scalar.activation(E[s], src, ACT.Exp, scale=scale).then_inc(done["gram_exp"], 1)
                    elif name == "aturn" and layer in (DIR_A, DIR_B):
                        wait_filled(act, it, step)
                        nc.scalar.activation(AT[s][:, 0].rearrange("p g k -> p (g k)"), bank_of(step)[:, 0:TOK],
                                             ACT.Copy).then_inc(done["aturn_dir"], 1)
                    elif name == "cnorm":
                        wait_for(act, it, "cshift", step)
                        for g in range(G):
                            src = bank_of((s, "context", layer, g))
                            sc = RI[s] if layer in (DIR_A, DIR_B) else RS[s]
                            nc.scalar.activation(HN[s][:, g], src[:, 0:D], ACT.Identity, bias=SH[s][:, g:g + 1],
                                                 scale=sc[:, g:g + 1]).then_inc(done["cnormed"], 1)
                    elif name == "finish":
                        wait_for(act, it, "y_biased", step)
                        n = it * STREAMS + s
                        act.dma_start(out_v[bass.ds(n, 1)].rearrange("a p g d -> (a p) g d"), HN[s][:]).then_inc(stored[s], 16)
            for s in range(STREAMS):
                act.wait_ge(stored[s], 16 * (ROUNDS + 1))

        @block.vector
        def _(v):
            handed = 0

            def hand_over(instruction, it):
                nonlocal handed
                handed += 1
                instruction.then_inc(vector_step, 1)
                v.wait_ge(vector_step, it * VECTOR_HANDOVERS + handed)

            v.wait_ge(rows_in, 48)
            nc.vector.tensor_scalar(bias_qk[:], bias_qk[:], WS, None, ALU.mult).then_inc(vector_setup, 1)
            for w in range(N_W):
                v.wait_ge(w_hi_done, w + 1)
                nc.vector.scalar_tensor_tensor(out=w_lo[:, w], in0=stage[w % 4], scalar=WS, in1=w_hi[:, w],
                                               op0=ALU.mult, op1=ALU.subtract).then_inc(w_lo_done, 1)
            v.wait_ge(w_lo_done, N_W)
            v.wait_ge(vector_setup, 1)
            v.wait_ge(consts_done, 1)
            for s in range(STREAMS):
                v.sem_inc(x_free[s], 1)
                v.sem_inc(stored[s], 16)
            start_ahead(v, "vector")
            v.sem_inc(setup_done, 1)

            def low_half(out, src, hi):
                return nc.vector.tensor_tensor(out, src, hi, ALU.subtract)

            with v.Fori(0, ROUNDS) as it:
                handed = 0
                for step in steps:
                    s, name, layer, i = step
                    if name == "load":
                        v.wait_ge(x_in[s], it * 32 + 32)
                        a = A[s][:]
                        hand_over(nc.vector.tensor_scalar(B0[s][:], a, 0.0, MASKED, ALU.is_le, ALU.mult), it)
                        nc.vector.scalar_tensor_tensor(out=B0[s][:], in0=a, scalar=beta_col[:, 0:1], in1=B0[s][:],
                                                       op0=ALU.mult, op1=ALU.add)
                        nc.vector.tensor_tensor(AA[s][:, :, 0, :], a, tri_dir[:, 0, :].unsqueeze(1).broadcast_to((P, G, P)),
                                                ALU.mult)
                        wait_filled(v, it, step)
                        nc.vector.tensor_tensor(
                            AA[s][:, :, 1, :], bank_of(step)[:, 0:TOK].rearrange("p (g k) -> p g k", g=G),
                            tri_dir[:, 1, :].unsqueeze(1).broadcast_to((P, G, P)), ALU.mult).then_inc(done["sides"], 1)
                    elif name == "stats":
                        if layer != GAT:
                            last = {DIR_A: (s, "back", GAT, G - 1), DIG_A: (s, "residual", DIR_B, None),
                                    GRAPHORMER: (s, "residual", DIG_B, None)}[layer]
                            wait_for(v, it, "x_added", last)
                        for g in range(G):
                            last = nc.vector.bn_stats(ST[s][:, g], X[s][:, g])
                        hand_over(last, it)
                        nc.vector.memset(pad_col[:], 0.0)
                        for g in range(G):
                            last = nc.vector.bn_aggr(MV[s][:, g], ST[s][:, g])
                        hand_over(last, it)
                        nc.vector.tensor_scalar(VE[s][:], MV[s][:, :, 1], 1e-5, None, ALU.add).then_inc(done["var"], 1)
                    elif name == "norm":
                        wait_for(v, it, "rstd", (s, "stats", layer, None))
                        nc.vector.scalar_tensor_tensor(out=SH[s][:], in0=MV[s][:, :, 0], scalar=-1.0, in1=RS[s][:],
                                                       op0=ALU.mult, op1=ALU.mult).then_inc(done["shift"], 1)
                    elif name == "turn":
                        wait_for(v, it, "turn_hi", step)
                        nc.vector.scalar_tensor_tensor(
                            out=HT[s][:, 1, :, i * P:(i + 1) * P], in0=bank_of(step)[:, 0:D].rearrange("p (c k) -> p c k", c=C),
                            scalar=0.0, in1=HT[s][:, 0, :, i * P:(i + 1) * P], op0=ALU.max,
                            op1=ALU.subtract).then_inc(done["turn_lo"], 1)
                    elif name == "proj":
                        wait_for(v, it, "proj_hi", step)
                        if layer == GAT:
                            for side in range(2):
                                last = nc.vector.scalar_tensor_tensor(
                                    out=QK[s][:, 1, i, side], in0=bank_of(step)[:, side * TOK:(side + 1) * TOK],
                                    scalar=bias_qk[:, side, i:i + 1], in1=QK[s][:, 0, i, side], op0=ALU.add, op1=ALU.subtract)
                        else:
                            last = low_half(QK[s][:, 1, i].rearrange("p a t -> p (a t)"), bank_of(step)[:, :],
                                            QK[s][:, 0, i].rearrange("p a t -> p (a t)"))
                        last.then_inc(done["proj_lo"], 1)
                    elif name == "vals":
                        wait_filled(v, it, step)
                        j, g = i // G, i % G
                        dst = (V[s], V1[s], V2[s])[j]
                        nc.vector.scalar_tensor_tensor(out=dst[:, g], in0=bank_of(step)[:, 0:D], scalar=1.0 / WS,
                                                       in1=row[:, ROW_V[layer][j], :], op0=ALU.mult,
                                                       op1=ALU.add).then_inc(done["vals"], 1)
                    elif name == "scores":
                        edge = B0[s] if layer == GAT else A[s]
                        scale = (1.0 / HD ** 0.5 if layer == GAT else 1.0 / D ** 0.5) / (WS * WS)
                        heads = T[s][:, i].rearrange("p (c h) k -> p c h k", h=HPC)
                        for h in range(HPC):
                            wait_filled(v, it, step, h)
                            nc.vector.scalar_tensor_tensor(
                                out=heads[:, :, h, :], in0=bank_of(step, h)[:, 0:D].rearrange("p (c k) -> p c k", c=C),
                                scalar=scale, in1=edge[:, i, :].unsqueeze(1).broadcast_to((P, C, P)), op0=ALU.mult,
                                op1=ALU.add).then_inc(done["scored"], 1)
                        wait_for(v, it, "scored", step, HPC - 1)
                        if layer == GAT:
                            nc.vector.tensor_reduce(MX[s][:, i], T[s][:, i], AX_X, ALU.max).then_inc(done["logits"], 1)
                        else:
                            nc.vector.tensor_reduce(MX[s][:, i], T[s][:, i], AX_X, ALU.max)
                            hand_over(nc.vector.tensor_reduce(AM[s][:, i], T[s][:, i], AX_X, ALU.max,
                                                              apply_absolute_value=True), it)
                            hand_over(nc.vector.tensor_scalar(AM[s][:, i], AM[s][:, i], 0.0, PAD_SHIFT, ALU.is_equal,
                                                              ALU.mult), it)
                            nc.vector.tensor_tensor(MX[s][:, i], MX[s][:, i], AM[s][:, i], ALU.add).then_inc(done["logits"], 1)
                    elif name == "mix":
                        wait_filled(v, it, step, 1)
                        sums = bank_of(step, 1)[:, 0:D].rearrange("p (c k) -> p c k", c=C)
                        if layer == GRAPHORMER:
                            hand_over(nc.vector.tensor_scalar(RD[s][:], sums, 1e-30, None, ALU.max), it)
                            sums = RD[s][:]
                        hand_over(nc.vector.reciprocal(RD[s][:], sums), it)
                        nc.vector.tensor_tensor(OT[s][:], bank_of(step, 0)[:, 0:D].rearrange("p (c k) -> p c k", c=C),
                                                RD[s][:], ALU.mult).then_inc(done["mixed"], 1)
                        if layer == GRAPHORMER:
                            wait_for(v, it, "mixed_hi", step)
                            low_half(OHL[s][:, 1], OT[s][:], OHL[s][:, 0]).then_inc(done["mixed_lo"], 1)
                    elif name == "back":
                        wait_filled(v, it, step)
                        nc.vector.tensor_tensor(X[s][:, i], bank_of(step)[:, 0:D], X[s][:, i],
                                                ALU.add).then_inc(done["x_added"], 1)
                    elif name == "project":
                        wait_filled(v, it, step)
                        nc.vector.scalar_tensor_tensor(out=HN[s][:, i], in0=bank_of(step)[:, 0:D], scalar=1.0 / WS,
                                                       in1=X[s][:, i], op0=ALU.mult, op1=ALU.add).then_inc(done["y"], 1)
                        if i == G - 1:
                            wait_for(v, it, "y", step)
                            v.sem_inc(x_free[s], 1)
                    elif name == "gram":
                        wait_filled(v, it, step)
                        if layer in (DIR_A, DIR_B):
                            hand_over(nc.vector.tensor_tensor(
                                U2[s].rearrange("p g w k -> p (g w k)"), bank_of(step)[:, :],
                                AA[s][:].rearrange("p g w k -> p (g w k)"), ALU.mult), it)
                            nc.vector.tensor_tensor(UW[s], U2[s][:, :, 0], U2[s][:, :, 1], ALU.add).then_inc(done["gram"], 1)
                        else:
                            u = bank_of(step)[:, 0:TOK].rearrange("p (g k) -> p g k", g=G)
                            hand_over(nc.vector.tensor_reduce(SE[s][:], u, AX_X, ALU.max), it)
                            nc.vector.tensor_tensor(UW2[s], u, SE[s][:].unsqueeze(2).broadcast_to((P, G, P)),
                                                    ALU.subtract).then_inc(done["gram"], 1)
                    elif name == "soft":
                        wait_for(v, it, "gram_exp", (s, "gram", layer, None))
                        if layer in (DIG_A, DIG_B):
                            nc.vector.tensor_reduce(SE[s][:], E[s], AX_X, ALU.add)
                        hand_over(nc.vector.tensor_tensor(DL[s], E[s], A[s][:], ALU.mult), it)
                        hand_over(nc.vector.tensor_reduce(SD[s][:], DL[s], AX_X, ALU.add), it)
                        if layer in (DIG_A, DIG_B):
                            hand_over(nc.vector.scalar_tensor_tensor(out=SD[s][:], in0=SE[s][:], scalar=1e-10, in1=SD[s][:],
                                                                     op0=ALU.mult, op1=ALU.add), it)
                        else:
                            hand_over(nc.vector.tensor_scalar(SD[s][:], SD[s][:], 1e-10, None, ALU.add), it)
                        hand_over(nc.vector.reciprocal(SR[s][:], SD[s][:]), it)
                        nc.vector.tensor_tensor(DL[s], DL[s], SR[s][:].unsqueeze(2).broadcast_to((P, G, P)),
                                                ALU.mult).then_inc(done["soft"], 1)
                    elif name == "aturn" and layer in (DIG_A, DIG_B):
                        wait_filled(v, it, step)
                        for w in range(3):
                            last = nc.vector.tensor_tensor(
                                AT[s][:, w], bank_of(step)[:, 0:TOK].rearrange("p (g k) -> p g k", g=G),
                                tri_dig[:, w, :].unsqueeze(1).broadcast_to((P, G, P)), ALU.mult)
                        last.then_inc(done["aturn_dig"], 1)
                    elif name == "context":
                        wait_filled(v, it, step)
                        hand_over(nc.vector.bn_stats(ST[s][:, i], bank_of(step)[:, 0:D]), it)
                    elif name == "cnorm":
                        nc.vector.memset(pad_col[:], 0.0)
                        for g in range(G):
                            last = nc.vector.bn_aggr(MV[s][:, g], ST[s][:, g])
                        hand_over(last, it)
                        if layer in (DIR_A, DIR_B):
                            nc.vector.tensor_scalar(VE[s][:], MV[s][:, :, 1], D / (D - 1.0), 1e-30, ALU.mult,
                                                    ALU.max).then_inc(done["cvar"], 1)
                            wait_for(v, it, "crstd", step)
                            hand_over(nc.vector.tensor_scalar(SR[s][:], RS[s][:], 1e-3, None, ALU.add), it)
                            hand_over(nc.vector.reciprocal(RI[s][:], SR[s][:]), it)
                            over = RI[s][:]
                        else:
                            nc.vector.tensor_scalar(VE[s][:], MV[s][:, :, 1], 1e-12, None, ALU.add).then_inc(done["cvar"], 1)
                            wait_for(v, it, "crstd", step)
                            over = RS[s][:]
                        nc.vector.scalar_tensor_tensor(out=SH[s][:], in0=MV[s][:, :, 0], scalar=-1.0, in1=over,
                                                       op0=ALU.mult, op1=ALU.mult).then_inc(done["cshift"], 1)
                    elif name == "residual":
                        wait_for(v, it, "affine", (s, "cnorm", layer, None))
                        nc.vector.scalar_tensor_tensor(out=X[s][:], in0=HN[s][:], scalar=0.0, in1=X[s][:], op0=ALU.max,
                                                       op1=ALU.add).then_inc(done["x_added"], 1)
                assert handed == VECTOR_HANDOVERS, handed

        @block.tensor
        def _(pe):
            pe.wait_ge(consts_done, 1)
            pe.wait_ge(setup_done, 1)

            def product(out, left, right, first=True, last=True):
                n = 0
                for (lh, ll), (rh, rl) in zip(left, right):
                    for a, b in ((lh, rh), (lh, rl), (ll, rh)):
                        m = nc.tensor.matmul(out, a, b, start=(first and n == 0), stop=(last and n == 3 * len(left) - 1))
                        n += 1
                return m

            def weight(w, c, cols=slice(0, D)):
                return w_hi[:, w, c, cols], w_lo[:, w, c, cols]

            def turned(s, c, cols=slice(0, TOK)):
                return HT[s][:, 0, c, cols], HT[s][:, 1, c, cols]

            with pe.Fori(0, ROUNDS) as it:
                for step in steps:
                    s, name, layer, i = step
                    for j in range(banks_of(name)):
                        wait_emptied(pe, it, step, j)
                    if name == "load":
                        pe.wait_ge(x_in[s], it * 32 + 32)
                        for g in range(G):
                            last = nc.tensor.transpose(bank_of(step)[:, g * P:(g + 1) * P], A[s][:, g], ident[:])
                        last.then_inc(filled, 1)
                    elif name == "turn":
                        if layer in (DIR_B, DIG_B):
                            wait_for(pe, it, "affine", (s, "cnorm", layer - 1, None))
                        else:
                            wait_for(pe, it, "normed", (s, "norm", layer, None), i)
                        for c in range(C):
                            last = nc.tensor.transpose(bank_of(step)[:, c * P:(c + 1) * P], HN[s][:, i, c * P:(c + 1) * P],
                                                       ident[:])
                        last.then_inc(filled, 1)
                    elif name == "proj":
                        wait_for(pe, it, "turn_lo", (s, "turn", layer, G - 1))
                        for side in range(2):
                            last = product(bank_of(step)[:, side * TOK:(side + 1) * TOK],
                                           [weight(W0[layer] + side, c, slice(i * P, (i + 1) * P)) for c in range(C)],
                                           [turned(s, c) for c in range(C)])
                        last.then_inc(filled, 1)
                    elif name == "vals":
                        j, g = i // G, i % G
                        wait_for(pe, it, "turn_lo", (s, "turn", layer, g))
                        w = W0[layer] + (j if layer in (DIG_A, DIG_B) else 2)
                        product(bank_of(step)[:, 0:D], [turned(s, c, slice(g * P, (g + 1) * P)) for c in range(C)],
                                [weight(w, c) for c in range(C)]).then_inc(filled, 1)
                    elif name == "scores":
                        wait_for(pe, it, "proj_lo", (s, "proj", layer, C - 1))
                        cols = slice(i * P, (i + 1) * P)
                        for c in range(C):
                            for n, (a, b) in enumerate(((0, 0), (0, 1), (1, 0))):
                                for h in range(HPC):
                                    rows_h = slice(HD * h, HD * (h + 1))
                                    m = nc.tensor.matmul(bank_of(step, h)[:, c * P:(c + 1) * P], QK[s][rows_h, a, c, 0, cols],
                                                         QK[s][rows_h, b, c, 1, cols], start=(n == 0), stop=(n == 2))
                                    if c == C - 1 and n == 2:
                                        m.then_inc(filled, 1)
                    elif name == "flip":
                        g, c = i
                        wait_for(pe, it, "centred", (s, "scores", layer, g))
                        for h in range(HPC):
                            last = nc.tensor.transpose(bank_of(step)[:, h * P:(h + 1) * P], T[s][:, g, HPC * c + h], ident[:])
                        last.then_inc(filled, 1)
                    elif name == "mix":
                        for c in range(C):
                            wait_for(pe, it, "probs", (s, "flip", layer, (i, c)))
                            if c == 0:
                                wait_for(pe, it, "vals", (s, "vals", layer, i))
                            for j in range(2):
                                for h in range(HPC):
                                    n = HPC * c + h
                                    left = V[s][:, i, HD * n:HD * (n + 1)] if j == 0 else ones[:]
                                    m = nc.tensor.matmul(bank_of(step, j)[HD * h:HD * (h + 1), c * P:(c + 1) * P], left,
                                                         PT[s][:, n], start=True, stop=True)
                                if c == C - 1:
                                    m.then_inc(filled, 1)
                    elif name == "back":
                        wait_for(pe, it, "mixed", (s, "mix", layer, i))
                        for c in range(C):
                            last = nc.tensor.transpose(bank_of(step)[:, c * P:(c + 1) * P], OT[s][:, c], ident[:])
                        last.then_inc(filled, 1)
                    elif name == "project":
                        wait_for(pe, it, "mixed_lo", (s, "mix", layer, i))
                        product(bank_of(step)[:, 0:D], [(OHL[s][:, 0, c], OHL[s][:, 1, c]) for c in range(C)],
                                [weight(W0[layer] + 3, c) for c in range(C)]).then_inc(filled, 1)
                    elif name == "gram":
                        if layer in (DIR_A, DIR_B):
                            wait_for(pe, it, "proj_lo", (s, "proj", layer, C - 1))
                            for g in range(G):
                                cols = slice(g * P, (g + 1) * P)
                                last = product(bank_of(step)[:, g * TOK:(g + 1) * TOK].rearrange("p (w k) -> p w k", w=2),
                                               [turned(s, c, cols) for c in range(C)],
                                               [(QK[s][:, 0, c, :, cols], QK[s][:, 1, c, :, cols]) for c in range(C)])
                        else:
                            wait_for(pe, it, "turn_lo", (s, "turn", layer, G - 1))
                            for g in range(G):
                                pair = [turned(s, c, slice(g * P, (g + 1) * P)) for c in range(C)]
                                last = product(bank_of(step)[:, g * P:(g + 1) * P], pair, pair)
                        last.then_inc(filled, 1)
                    elif name == "aturn":
                        wait_for(pe, it, "soft", (s, "soft", layer, None))
                        for g in range(G):
                            last = nc.tensor.transpose(bank_of(step)[:, g * P:(g + 1) * P], DL[s][:, g], ident[:])
                        last.then_inc(filled, 1)
                    elif name == "context":
                        kinds = len(ROW_V[layer])
                        wait_for(pe, it, "aturn_dir" if layer in (DIR_A, DIR_B) else "aturn_dig", (s, "aturn", layer, None))
                        wait_for(pe, it, "vals", (s, "vals", layer, (kinds - 1) * G + i))
                        for j in range(kinds):
                            last = nc.tensor.matmul(bank_of(step)[:, 0:D], AT[s][:, j, i], (V[s], V1[s], V2[s])[j][:, i],
                                                    start=(j == 0), stop=(j == kinds - 1))
                        last.then_inc(filled, 1)


_MATRICES = [("L0_gnn_Wq", None), ("L0_gnn_Wk", None), ("L0_gnn_Wv", None),
             ("L1_gnn_W_left", 0), ("L1_gnn_W_right", 0), ("L1_gnn_W_lin", 0),
             ("L1_gnn_W_left", 1), ("L1_gnn_W_right", 1), ("L1_gnn_W_lin", 1),
             ("L2_gnn_Wl", 0), ("L2_gnn_Ws", 0), ("L2_gnn_Wr", 0), ("L2_gnn_Wl", 1), ("L2_gnn_Ws", 1), ("L2_gnn_Wr", 1),
             ("L3_gnn_Wq", None), ("L3_gnn_Wk", None), ("L3_gnn_Wv", None), ("L3_gnn_Wo", None)]
_ROWS = [("L0_gnn_bv", None), ("L1_gnn_b_lin", 0), ("L1_gnn_b_lin", 1),
         ("L2_gnn_bl", 0), ("L2_gnn_bs", 0), ("L2_gnn_br", 0), ("L2_gnn_bl", 1), ("L2_gnn_bs", 1), ("L2_gnn_br", 1),
         ("L3_gnn_bv", None), ("L3_gnn_bo", None),
         ("L1_gnn_ln_a", 0), ("L1_gnn_ln_b", 0), ("L1_gnn_ln_a", 1), ("L1_gnn_ln_b", 1),
         ("L2_gnn_ln_w", 0), ("L2_gnn_ln_b", 0), ("L2_gnn_ln_w", 1), ("L2_gnn_ln_b", 1)]


def layout(inputs):
    import numpy as np

    def pick(name, at):
        a = np.asarray(inputs[name])
        return a if at is None else a[at]

    weights = np.stack([pick(n, at) if n.startswith("L0") else pick(n, at).T for n, at in _MATRICES])
    rows = np.stack([pick(n, at) for n, at in _ROWS])
    qk = np.stack([np.asarray(inputs["L0_gnn_bq"]).reshape(C, P), np.asarray(inputs["L0_gnn_bk"]).reshape(C, P)])
    return {"x": np.ascontiguousarray(inputs["x"]), "adj": np.ascontiguousarray(inputs["adj"]),
            "weights": np.ascontiguousarray(weights), "rows": np.ascontiguousarray(rows),
            "qk_bias": np.ascontiguousarray(qk.transpose(2, 0, 1)), "beta": np.asarray(inputs["L0_gnn_beta"]).reshape(1)}


def kernel(**inputs):
    import concourse.bacc as _bacc
    from concourse import mybir as _mybir
    from concourse.bass_utils import run_bass_kernel_spmd as _run

    nc = _bacc.Bacc("TRN2", target_bir_lowering=False, num_devices=1)
    arrays, args = {}, []
    for name, a in layout(inputs).items():
        arrays[f"in_{name}_dram"] = a
        args.append(nc.dram_tensor(f"in_{name}_dram", a.shape, _mybir.dt.from_np(a.dtype), kind="ExternalInput").ap())
    args.append(nc.dram_tensor("out_dram", arrays["in_x_dram"].shape, F32, kind="ExternalOutput").ap())
    graph_layers_kernel(nc, *args)
    r = _run(nc, [arrays], core_ids=[0])
    return r.results[0]["out_dram"]
```

```python
from contextlib import ExitStack

import concourse.bass as bass
from concourse import mybir

ALU = mybir.AluOpType
ACT = mybir.ActivationFunctionType
AX_X = mybir.AxisListType.X
F32 = mybir.dt.float32
F16 = mybir.dt.float16

P = 128
D = 384
C = D // P
G = 2
STREAMS = 2
TOK = G * P
H = 12
HD = D // H
HPC = P // HD
BANKS = 4
WS = 16.0

GAT, DIR_A, DIR_B, DIG_A, DIG_B, GRAPHORMER = range(6)
ATTENTION = (GAT, GRAPHORMER)
W0 = {GAT: 0, DIR_A: 3, DIR_B: 6, DIG_A: 9, DIG_B: 12, GRAPHORMER: 15}
N_W = 19
ROW_V = {GAT: [0], DIR_A: [1], DIR_B: [2], DIG_A: [3, 4, 5], DIG_B: [6, 7, 8], GRAPHORMER: [9]}
ROW_BO = 10
ROW_LN = {DIR_A: 11, DIR_B: 13, DIG_A: 15, DIG_B: 17}
N_ROWS = 19
MASKED = -9000000000000000.0
PAD_SHIFT = 1.0e5


def stream_steps():
    out = []

    def add(name, layer=None, i=None):
        out.append((name, layer, i))

    add("load")
    for layer in range(6):
        if layer not in (DIR_B, DIG_B):
            add("stats", layer)
            add("shift", layer)
            for g in range(G):
                add("norm", layer, g)
        for g in range(G):
            add("turn", layer, g)
        if layer in ATTENTION or layer in (DIR_A, DIR_B):
            for m in range(C):
                add("proj", layer, m)
        if layer in ATTENTION:
            for g in range(G):
                add("vals", layer, g)
            for g in range(G):
                add("scores", layer, g)
            for g in range(G):
                for c in range(C):
                    add("flip", layer, (g, c))
                add("mix", layer, g)
                if layer == GRAPHORMER:
                    add("halve", layer, g)
                if layer == GAT:
                    add("back", layer, g)
                else:
                    add("project", layer, g)
        else:
            add("gram", layer)
            for j in range(len(ROW_V[layer])):
                for g in range(G):
                    add("vals", layer, j * G + g)
                if j == 0:
                    add("soft", layer)
            add("aturn", layer)
            for g in range(G):
                add("context", layer, g)
            add("cstats", layer)
            add("cshift", layer)
            for g in range(G):
                add("cnorm", layer, g)
            add("affine", layer)
            if layer in (DIR_B, DIG_B):
                add("residual", layer)
    add("finish")
    return out


TURNS = {
    "tensor": ("011000000011011110100010100001110101111001000100010001111110010001000100011111111100100000110001"
               "11001111001100000001100011111100111000001010111100011110110000011111101111"),
    "vector": ("001011010101010001101111011010010010100110001000011000101111110010001000010000101001001101000001"
               "1000111000011110011110000000010100001010101111001111010100101010111111111011101001101111101111"),
    "scalar": ("000011000111111100000011110011100100010011001111100000001110011100000111111100110011011001110010"
               "01110001111100001100011010"),
    "pool": "0111001101100110001001100011100110",
    "sync": "01",
}
LATE = {"tensor": 64, "vector": 73, "scalar": 43, "pool": 11, "sync": 1}


def banks_of(name):
    return {"load": 1, "turn": 1, "proj": 1, "vals": 1, "scores": HPC, "flip": 1, "mix": 2, "back": 1, "project": 1,
            "gram": 1, "aturn": 1, "context": 1}.get(name, 0)


def signals_of(step):
    name, layer, i = step
    directed = layer in (DIR_A, DIR_B)
    if name == "load":
        return ["handed", "sides"]
    if name == "stats":
        return ["handed"] * 2 + ["var", "rstd"]
    if name == "shift":
        return ["shift"]
    if name == "norm":
        return ["normed"]
    if name == "turn":
        return ["turn_hi", "turn_lo"]
    if name == "proj":
        return ["proj_hi", "proj_lo"]
    if name == "vals":
        return ["vals"]
    if name == "scores":
        return ["scored"] * HPC + ["handed"] * (2 if layer == GRAPHORMER else 0) + ["logits", "centred"]
    if name == "flip":
        return ["probs"]
    if name == "mix":
        return ["handed"] * (2 if layer == GRAPHORMER else 1) + ["mixed"]
    if name == "halve":
        return ["mixed_hi", "mixed_lo"]
    if name == "back":
        return ["x_added"]
    if name == "project":
        return ["y"]
    if name == "gram":
        return ["handed", "gram", "gram_exp"]
    if name == "soft":
        return ["handed"] * 4 + ["soft"]
    if name == "aturn":
        return ["aturn_dir" if directed else "aturn_dig"]
    if name == "context":
        return ["handed"]
    if name == "cstats":
        return ["handed", "cvar", "crstd"]
    if name == "cshift":
        return (["handed"] * 2 if directed else []) + ["cshift"]
    if name == "cnorm":
        return ["cnormed"]
    if name == "affine":
        return ["pool_handed", "affine"]
    if name == "residual":
        return ["x_added"]
    if name == "finish":
        return ["y_biased"]
    return []


def has_part(engine, step):
    name, layer, i = step
    directed = layer in (DIR_A, DIR_B)
    if engine == "tensor":
        return banks_of(name) > 0
    if engine == "vector":
        return name not in ("norm", "cnorm", "affine", "flip", "finish") and not (name == "aturn" and directed)
    if engine == "scalar":
        return (name in ("norm", "turn", "proj", "flip", "gram", "halve", "cnorm", "finish")
                or name == "aturn" and directed)
    if engine == "pool":
        return name in ("stats", "scores", "cstats", "affine", "finish")
    return name == "load"


RELEASE = {"load": "sides", "turn": "turn_lo", "proj": "proj_lo", "vals": "vals", "scores": "scored", "flip": "probs", "mix": "mixed",
           "back": "x_added", "project": "y", "gram": "gram", "context": "cnormed"}


def release_of(step, j):
    name, layer, i = step
    if name == "aturn":
        return "aturn_dir" if layer in (DIR_A, DIR_B) else "aturn_dig", step, 0
    if name == "context":
        return "cnormed", ("cnorm", layer, i), 0
    return RELEASE[name], step, j if name == "scores" else 0


class Plan:

    def __init__(self):
        self.steps = stream_steps()
        self.total, self.nth = {}, {}
        self.fills = 0
        self.bank = {}
        self.user = {}
        last = {}
        for step in self.steps:
            for sig in signals_of(step):
                self.nth.setdefault((sig, step), []).append(self.total.get(sig, 0))
                self.total[sig] = self.total.get(sig, 0) + 1
            self.bank[step] = []
            for j in range(banks_of(step[0])):
                b = self.fills % BANKS
                self.bank[step].append((b, self.fills))
                self.user[step, j] = (last.get(b), 0)
                last[b] = (step, j)
                self.fills += 1
        for key, (before, _) in self.user.items():
            if before is None:
                self.user[key] = (last[self.bank[key[0]][key[1]][0]], 1)




def graph_layers_kernel(nc, x, adj, weights, rows, qk_bias, beta, out):
    N = x.shape[0]
    ROUNDS = N // (G * STREAMS)
    plan = Plan()
    nc.disable_value_cache = True

    with ExitStack() as ctx:
        def sb(name, shape, dt=F32):
            return ctx.enter_context(nc.sbuf_tensor(name, shape, dt))

        def sem(name):
            return ctx.enter_context(nc.semaphore(name))

        w_hi = sb("w_hi", [P, N_W, C, D], F16)
        w_lo = sb("w_lo", [P, N_W, C, D], F16)
        row = sb("row", [P, N_ROWS, D])
        bias_qk = sb("bias_qk", [P, 2, C])
        beta_col = sb("beta_col", [P, 1])
        ident = sb("ident", [P, P])
        tri_dir = sb("tri_dir", [P, 2, P])
        tri_dig = sb("tri_dig", [P, 3, P])
        ones = sb("ones", [P, HD])
        powers = sb("powers", [P, 2, G])
        pad_col = sb("pad_col", [P, 1])

        X = [sb(f"x{s}", [P, G, D]) for s in range(STREAMS)]
        A = [sb(f"adj{s}", [P, G, P]) for s in range(STREAMS)]
        HN = [sb(f"h{s}", [P, G, D]) for s in range(STREAMS)]
        HT = [sb(f"ht{s}", [P, 2, C, TOK], F16) for s in range(STREAMS)]
        QK = [sb(f"qk{s}", [P, 2, C, 2, TOK], F16) for s in range(STREAMS)]
        V = [sb(f"v{s}", [P, G, D]) for s in range(STREAMS)]
        T = [sb(f"t{s}", [P, G, H, P]) for s in range(STREAMS)]
        PT = [sb(f"pt{s}", [P, H, P]) for s in range(STREAMS)]
        RD = [sb(f"rd{s}", [P, C, P]) for s in range(STREAMS)]
        OT = [sb(f"ot{s}", [P, C, P]) for s in range(STREAMS)]
        OHL = [sb(f"ohl{s}", [P, 2, C, P], F16) for s in range(STREAMS)]
        B0 = [sb(f"b0_{s}", [P, G, P]) for s in range(STREAMS)]
        AA = [sb(f"aa{s}", [P, G, 2, P]) for s in range(STREAMS)]
        ST = [sb(f"st{s}", [P, G, 6]) for s in range(STREAMS)]
        MV = [sb(f"mv{s}", [P, G, 2]) for s in range(STREAMS)]
        VE = [sb(f"ve{s}", [P, G]) for s in range(STREAMS)]
        RS = [sb(f"rs{s}", [P, G]) for s in range(STREAMS)]
        RI = [sb(f"ri{s}", [P, G]) for s in range(STREAMS)]
        SH = [sb(f"sh{s}", [P, G]) for s in range(STREAMS)]
        MX = [sb(f"mx{s}", [P, G, H]) for s in range(STREAMS)]
        AM = [sb(f"am{s}", [P, G, H]) for s in range(STREAMS)]
        SE = [sb(f"se{s}", [P, G]) for s in range(STREAMS)]
        SD = [sb(f"sd{s}", [P, G]) for s in range(STREAMS)]
        SR = [sb(f"sr{s}", [P, G]) for s in range(STREAMS)]

        flat = [T[s][:].rearrange("p g h k -> p (g h k)") for s in range(STREAMS)]
        V1 = [f[:, 0:768].rearrange("p (g d) -> p g d", g=G) for f in flat]
        V2 = [f[:, 768:1536].rearrange("p (g d) -> p g d", g=G) for f in flat]
        U2 = [f[:, 0:512].rearrange("p (g w k) -> p g w k", g=G, w=2) for f in flat]
        UW = [f[:, 512:768].rearrange("p (g k) -> p g k", g=G) for f in flat]
        UW2 = [f[:, 1536:1792].rearrange("p (g k) -> p g k", g=G) for f in flat]
        E = [f[:, 1792:2048].rearrange("p (g k) -> p g k", g=G) for f in flat]
        DL = [f[:, 2048:2304].rearrange("p (g k) -> p g k", g=G) for f in flat]
        AT = [f[:, 2304:3072].rearrange("p (w g k) -> p w g k", w=3, g=G) for f in flat]

        bank = [[ctx.enter_context(nc.psum_tensor(f"bank{s}_{b}", [P, 512], F32)) for b in range(BANKS)]
                for s in range(STREAMS)]

        done = [{name: sem(f"{name}{s}") for name in plan.total} for s in range(STREAMS)]
        filled = [sem(f"bank_filled{s}") for s in range(STREAMS)]
        x_in = [sem(f"x_in{s}") for s in range(STREAMS)]
        x_free = [sem(f"x_free{s}") for s in range(STREAMS)]
        stored = [sem(f"stored{s}") for s in range(STREAMS)]
        w_in = [sem(f"w_in{i}") for i in range(4)]
        w_hi_done, w_lo_done = sem("w_hi_done"), sem("w_lo_done")
        vector_setup = sem("vector_setup")
        rows_in, consts_done, setup_done = sem("rows_in"), sem("consts_done"), sem("setup_done")
        pool_setup = sem("pool_setup")

        x_v = x.rearrange("(n g) p d -> n p g d", g=G)
        adj_v = adj.rearrange("(n g) p k -> n p g k", g=G)
        out_v = out.rearrange("(n g) p d -> n p g d", g=G)
        w_v = weights.rearrange("w (c p) n -> w p c n", p=P)

        def count(r, total, nth):
            it, back = r
            return it * total + (nth + 1 - back * total)

        def first_round(r):
            return isinstance(r[0], int) and r[0] == r[1]

        def wait_for(eng, r, s, sig, step, n=0):
            eng.wait_ge(done[s][sig], count(r, plan.total[sig], plan.nth[sig, step][n]))

        def wait_filled(eng, r, s, step, j=0):
            eng.wait_ge(filled[s], count(r, plan.fills, plan.bank[step][j][1]))

        def wait_emptied(eng, r, s, step):
            need = {}
            for j in range(banks_of(step[0])):
                (before, k), ago = plan.user[step, j]
                sig, giver, n = release_of(before, k)
                need[sig] = (ago, plan.nth[sig, giver][n])
            for sig, (ago, nth) in need.items():
                it, back = r
                if isinstance(it, int) and it - back - ago < 0:
                    continue
                eng.wait_ge(done[s][sig], count((it, back + ago), plan.total[sig], nth))

        def bank_of(s, step, j=0):
            return bank[s][plan.bank[step][j][0]]

        def rounds(eng, engine, step_of):
            own = [x for x in plan.steps if has_part(engine, x)]
            late = LATE[engine]
            queues = [[(x, 0) for x in own], [(x, 1) for x in own[late:]] + [(x, 0) for x in own[:late]]]
            turns = []
            for s in map(int, TURNS[engine]):
                turns.append((s, *queues[s].pop(0)))
            assert not queues[0] and not queues[1], (engine, len(queues[0]), len(queues[1]))
            for s, step, back in turns:
                if not back:
                    step_of((0, 0), s, *step)
            with eng.Fori(1, ROUNDS) as it:
                for s, step, back in turns:
                    step_of((it, back), s, *step)
            for s, step, back in turns:
                if back:
                    step_of((ROUNDS, 1), s, *step)

        stage = [flat[i // 2][:, (i % 2) * 1536:(i % 2) * 1536 + C * D].rearrange("p (c n) -> p c n", c=C)
                 for i in range(4)]
        block = ctx.enter_context(nc.Block())

        @block.sync
        def _(sp):
            sp.dma_start(row[:], rows.rearrange("(a r) d -> a r d", a=1).broadcast_to((P, N_ROWS, D))).then_inc(rows_in, 16)
            sp.dma_start(bias_qk[:], qk_bias).then_inc(rows_in, 16)
            sp.dma_start(beta_col[:], beta.rearrange("(a b) -> a b", a=1).broadcast_to((P, 1))).then_inc(rows_in, 16)
            for w in range(N_W):
                if w >= 4:
                    sp.wait_ge(w_lo_done, w - 3)
                sp.dma_start(stage[w % 4], w_v[w]).then_inc(w_in[w % 4], 16)
            def step_of(r, s, name, layer, i):
                step = (name, layer, i)
                if name == "load":
                    if not first_round(r):
                        sp.wait_ge(x_free[s], r[0])
                    n = (r[0] - r[1]) * STREAMS + s
                    sp.dma_start(X[s][:], x_v[bass.ds(n, 1)].rearrange("a p g d -> (a p) g d")).then_inc(x_in[s], 16)
                    sp.dma_start(A[s][:], adj_v[bass.ds(n, 1)].rearrange("a p g d -> (a p) g d")).then_inc(x_in[s], 16)

            rounds(sp, "sync", step_of)

        @block.gpsimd
        def _(pool):
            n = 0

            def select(view, op, base, pattern, cm):
                nonlocal n
                nc.gpsimd.memset(view, 1.0).then_inc(pool_setup, 1)
                n += 1
                pool.wait_ge(pool_setup, n)
                return nc.gpsimd.affine_select(out=view, in_=view, compare_op=op, fill=0.0, base=base,
                                               pattern=[[pattern, P]], channel_multiplier=cm)

            select(ident[:], ALU.is_equal, 0, -1, 1)
            select(tri_dir[:, 0, :], ALU.is_ge, 0, 1, -1)
            select(tri_dir[:, 1, :], ALU.is_ge, -1, -1, 1)
            select(tri_dig[:, 0, :], ALU.is_ge, -1, -1, 1)
            select(tri_dig[:, 1, :], ALU.is_equal, 0, -1, 1)
            select(tri_dig[:, 2, :], ALU.is_ge, -1, 1, -1)
            nc.gpsimd.memset(powers[:, 0, :], -0.5)
            nc.gpsimd.memset(powers[:, 1, :], 0.5)
            nc.gpsimd.memset(ones[:], 1.0).then_inc(consts_done, 1)
            pool.wait_ge(consts_done, 1)
            pool.wait_ge(rows_in, 48)
            def step_of(r, s, name, layer, i):
                step = (name, layer, i)
                if name == "stats":
                    wait_for(pool, r, s, "var", step)
                    nc.gpsimd.tensor_tensor(RS[s][:], VE[s][:], powers[:, 0, :], ALU.pow).then_inc(done[s]["rstd"], 1)
                elif name == "scores":
                    wait_for(pool, r, s, "logits", step)
                    nc.gpsimd.tensor_tensor(T[s][:, i], T[s][:, i],
                                            MX[s][:, i, :].unsqueeze(2).broadcast_to((P, H, P)),
                                            ALU.subtract).then_inc(done[s]["centred"], 1)
                elif name == "cstats":
                    wait_for(pool, r, s, "cvar", step)
                    which = 1 if layer in (DIR_A, DIR_B) else 0
                    nc.gpsimd.tensor_tensor(RS[s][:], VE[s][:], powers[:, which, :], ALU.pow).then_inc(done[s]["crstd"], 1)
                elif name == "affine":
                    wait_for(pool, r, s, "cnormed", ("cnorm", layer, G - 1))
                    at = ROW_LN[layer]
                    nc.gpsimd.tensor_tensor(HN[s][:], HN[s][:], row[:, at, :].unsqueeze(1).broadcast_to((P, G, D)),
                                            ALU.mult).then_inc(done[s]["pool_handed"], 1)
                    wait_for(pool, r, s, "pool_handed", step)
                    nc.gpsimd.tensor_tensor(HN[s][:], HN[s][:],
                                            row[:, at + 1, :].unsqueeze(1).broadcast_to((P, G, D)),
                                            ALU.add).then_inc(done[s]["affine"], 1)
                elif name == "finish":
                    last = ("project", GRAPHORMER, G - 1)
                    wait_for(pool, r, s, "y", last)
                    nc.gpsimd.tensor_tensor(HN[s][:], HN[s][:],
                                            row[:, ROW_BO, :].unsqueeze(1).broadcast_to((P, G, D)),
                                            ALU.add).then_inc(done[s]["y_biased"], 1)

            rounds(pool, "pool", step_of)

        @block.scalar
        def _(act):
            for w in range(N_W):
                act.wait_ge(w_in[w % 4], 16 * (w // 4 + 1))
                nc.scalar.activation(w_hi[:, w], stage[w % 4], ACT.Copy, scale=WS).then_inc(w_hi_done, 1)
            act.wait_ge(setup_done, 1)
            def step_of(r, s, name, layer, i):
                step = (name, layer, i)
                if name == "norm":
                    wait_for(act, r, s, "shift", ("shift", layer, None))
                    if layer == GAT and i == 0 and not first_round(r):
                        act.wait_ge(stored[s], r[0] * 16)
                    nc.scalar.activation(HN[s][:, i], X[s][:, i], ACT.Identity, bias=SH[s][:, i:i + 1],
                                         scale=RS[s][:, i:i + 1]).then_inc(done[s]["normed"], 1)
                elif name == "turn":
                    wait_filled(act, r, s, step)
                    nc.scalar.activation(HT[s][:, 0, :, i * P:(i + 1) * P],
                                         bank_of(s, step)[:, 0:D].rearrange("p (c k) -> p c k", c=C),
                                         ACT.Relu).then_inc(done[s]["turn_hi"], 1)
                elif name == "proj":
                    wait_filled(act, r, s, step)
                    if layer == GAT:
                        for side in range(2):
                            last = nc.scalar.activation(QK[s][:, 0, i, side], bank_of(s, step)[:, side * TOK:(side + 1) * TOK],
                                                        ACT.Identity, bias=bias_qk[:, side, i:i + 1])
                    else:
                        last = nc.scalar.activation(QK[s][:, 0, i].rearrange("p a t -> p (a t)"), bank_of(s, step)[:, :], ACT.Copy)
                    last.then_inc(done[s]["proj_hi"], 1)
                elif name == "flip":
                    g, c = i
                    wait_filled(act, r, s, step)
                    nc.scalar.activation(PT[s][:, HPC * c:HPC * (c + 1)].rearrange("p h k -> p (h k)"),
                                         bank_of(s, step)[:, :], ACT.Exp).then_inc(done[s]["probs"], 1)
                elif name == "halve":
                    wait_for(act, r, s, "mixed", ("mix", layer, i))
                    nc.scalar.activation(OHL[s][:, 0], OT[s][:], ACT.Copy).then_inc(done[s]["mixed_hi"], 1)
                elif name == "gram":
                    wait_for(act, r, s, "gram", step)
                    src = UW[s] if layer in (DIR_A, DIR_B) else UW2[s]
                    scale = 1.0 / (WS * D ** 0.5) if layer in (DIR_A, DIR_B) else 1.0 / D ** 0.5
                    nc.scalar.activation(E[s], src, ACT.Exp, scale=scale).then_inc(done[s]["gram_exp"], 1)
                elif name == "aturn" and layer in (DIR_A, DIR_B):
                    wait_filled(act, r, s, step)
                    nc.scalar.activation(AT[s][:, 0].rearrange("p g k -> p (g k)"), bank_of(s, step)[:, 0:TOK],
                                         ACT.Copy).then_inc(done[s]["aturn_dir"], 1)
                elif name == "cnorm":
                    wait_for(act, r, s, "cshift", ("cshift", layer, None))
                    scale = RI[s] if layer in (DIR_A, DIR_B) else RS[s]
                    nc.scalar.activation(HN[s][:, i], bank_of(s, ("context", layer, i))[:, 0:D], ACT.Identity,
                                         bias=SH[s][:, i:i + 1], scale=scale[:, i:i + 1]).then_inc(done[s]["cnormed"], 1)
                elif name == "finish":
                    wait_for(act, r, s, "y_biased", step)
                    n = (r[0] - r[1]) * STREAMS + s
                    act.dma_start(out_v[bass.ds(n, 1)].rearrange("a p g d -> (a p) g d"), HN[s][:]).then_inc(stored[s], 16)

            rounds(act, "scalar", step_of)
            for s in range(STREAMS):
                act.wait_ge(stored[s], 16 * ROUNDS)

        @block.vector
        def _(v):
            def hand_over(instruction, r, s, step, n):
                instruction.then_inc(done[s]["handed"], 1)
                wait_for(v, r, s, "handed", step, n)

            v.wait_ge(rows_in, 48)
            nc.vector.tensor_scalar(bias_qk[:], bias_qk[:], WS, None, ALU.mult).then_inc(vector_setup, 1)
            for w in range(N_W):
                v.wait_ge(w_hi_done, w + 1)
                nc.vector.scalar_tensor_tensor(out=w_lo[:, w], in0=stage[w % 4], scalar=WS, in1=w_hi[:, w],
                                               op0=ALU.mult, op1=ALU.subtract).then_inc(w_lo_done, 1)
            v.wait_ge(w_lo_done, N_W)
            v.wait_ge(vector_setup, 1)
            v.wait_ge(consts_done, 1)
            v.sem_inc(setup_done, 1)

            def low_half(out, src, hi):
                return nc.vector.tensor_tensor(out, src, hi, ALU.subtract)

            def step_of(r, s, name, layer, i):
                step = (name, layer, i)
                if name == "load":
                    v.wait_ge(x_in[s], r[0] * 32 + 32)
                    a = A[s][:]
                    hand_over(nc.vector.tensor_scalar(B0[s][:], a, 0.0, MASKED, ALU.is_le, ALU.mult), r, s, step, 0)
                    nc.vector.scalar_tensor_tensor(out=B0[s][:], in0=a, scalar=beta_col[:, 0:1], in1=B0[s][:],
                                                   op0=ALU.mult, op1=ALU.add)
                    nc.vector.tensor_tensor(AA[s][:, :, 0, :], a, tri_dir[:, 0, :].unsqueeze(1).broadcast_to((P, G, P)),
                                            ALU.mult)
                    wait_filled(v, r, s, step)
                    nc.vector.tensor_tensor(
                        AA[s][:, :, 1, :], bank_of(s, step)[:, 0:TOK].rearrange("p (g k) -> p g k", g=G),
                        tri_dir[:, 1, :].unsqueeze(1).broadcast_to((P, G, P)), ALU.mult).then_inc(done[s]["sides"], 1)
                elif name == "stats":
                    if layer != GAT:
                        last = {DIR_A: ("back", GAT, G - 1), DIG_A: ("residual", DIR_B, None),
                                GRAPHORMER: ("residual", DIG_B, None)}[layer]
                        wait_for(v, r, s, "x_added", last)
                    for g in range(G):
                        last = nc.vector.bn_stats(ST[s][:, g], X[s][:, g])
                    hand_over(last, r, s, step, 0)
                    nc.vector.memset(pad_col[:], 0.0)
                    for g in range(G):
                        last = nc.vector.bn_aggr(MV[s][:, g], ST[s][:, g])
                    hand_over(last, r, s, step, 1)
                    nc.vector.tensor_scalar(VE[s][:], MV[s][:, :, 1], 1e-5, None, ALU.add).then_inc(done[s]["var"], 1)
                elif name == "shift":
                    wait_for(v, r, s, "rstd", ("stats", layer, None))
                    nc.vector.scalar_tensor_tensor(out=SH[s][:], in0=MV[s][:, :, 0], scalar=-1.0, in1=RS[s][:],
                                                   op0=ALU.mult, op1=ALU.mult).then_inc(done[s]["shift"], 1)
                elif name == "turn":
                    wait_for(v, r, s, "turn_hi", step)
                    nc.vector.scalar_tensor_tensor(
                        out=HT[s][:, 1, :, i * P:(i + 1) * P], in0=bank_of(s, step)[:, 0:D].rearrange("p (c k) -> p c k", c=C),
                        scalar=0.0, in1=HT[s][:, 0, :, i * P:(i + 1) * P], op0=ALU.max,
                        op1=ALU.subtract).then_inc(done[s]["turn_lo"], 1)
                elif name == "proj":
                    wait_for(v, r, s, "proj_hi", step)
                    if layer == GAT:
                        for side in range(2):
                            last = nc.vector.scalar_tensor_tensor(
                                out=QK[s][:, 1, i, side], in0=bank_of(s, step)[:, side * TOK:(side + 1) * TOK],
                                scalar=bias_qk[:, side, i:i + 1], in1=QK[s][:, 0, i, side], op0=ALU.add, op1=ALU.subtract)
                    else:
                        last = low_half(QK[s][:, 1, i].rearrange("p a t -> p (a t)"), bank_of(s, step)[:, :],
                                        QK[s][:, 0, i].rearrange("p a t -> p (a t)"))
                    last.then_inc(done[s]["proj_lo"], 1)
                elif name == "vals":
                    wait_filled(v, r, s, step)
                    j, g = i // G, i % G
                    dst = (V[s], V1[s], V2[s])[j]
                    nc.vector.scalar_tensor_tensor(out=dst[:, g], in0=bank_of(s, step)[:, 0:D], scalar=1.0 / WS,
                                                   in1=row[:, ROW_V[layer][j], :], op0=ALU.mult,
                                                   op1=ALU.add).then_inc(done[s]["vals"], 1)
                elif name == "scores":
                    edge = B0[s] if layer == GAT else A[s]
                    scale = (1.0 / HD ** 0.5 if layer == GAT else 1.0 / D ** 0.5) / (WS * WS)
                    heads = T[s][:, i].rearrange("p (c h) k -> p c h k", h=HPC)
                    for h in range(HPC):
                        wait_filled(v, r, s, step, h)
                        nc.vector.scalar_tensor_tensor(
                            out=heads[:, :, h, :], in0=bank_of(s, step, h)[:, 0:D].rearrange("p (c k) -> p c k", c=C),
                            scalar=scale, in1=edge[:, i, :].unsqueeze(1).broadcast_to((P, C, P)), op0=ALU.mult,
                            op1=ALU.add).then_inc(done[s]["scored"], 1)
                    wait_for(v, r, s, "scored", step, HPC - 1)
                    if layer == GAT:
                        nc.vector.tensor_reduce(MX[s][:, i], T[s][:, i], AX_X, ALU.max).then_inc(done[s]["logits"], 1)
                    else:
                        nc.vector.tensor_reduce(MX[s][:, i], T[s][:, i], AX_X, ALU.max)
                        hand_over(nc.vector.tensor_reduce(AM[s][:, i], T[s][:, i], AX_X, ALU.max,
                                                          apply_absolute_value=True), r, s, step, 0)
                        hand_over(nc.vector.tensor_scalar(AM[s][:, i], AM[s][:, i], 0.0, PAD_SHIFT, ALU.is_equal,
                                                          ALU.mult), r, s, step, 1)
                        nc.vector.tensor_tensor(MX[s][:, i], MX[s][:, i], AM[s][:, i], ALU.add).then_inc(done[s]["logits"], 1)
                elif name == "mix":
                    wait_filled(v, r, s, step, 1)
                    sums = bank_of(s, step, 1)[:, 0:D].rearrange("p (c k) -> p c k", c=C)
                    if layer == GRAPHORMER:
                        hand_over(nc.vector.tensor_scalar(RD[s][:], sums, 1e-30, None, ALU.max), r, s, step, 0)
                        sums = RD[s][:]
                    hand_over(nc.vector.reciprocal(RD[s][:], sums), r, s, step, 1 if layer == GRAPHORMER else 0)
                    nc.vector.tensor_tensor(OT[s][:], bank_of(s, step, 0)[:, 0:D].rearrange("p (c k) -> p c k", c=C),
                                            RD[s][:], ALU.mult).then_inc(done[s]["mixed"], 1)
                elif name == "halve":
                    wait_for(v, r, s, "mixed_hi", step)
                    low_half(OHL[s][:, 1], OT[s][:], OHL[s][:, 0]).then_inc(done[s]["mixed_lo"], 1)
                elif name == "back":
                    wait_filled(v, r, s, step)
                    nc.vector.tensor_tensor(X[s][:, i], bank_of(s, step)[:, 0:D], X[s][:, i],
                                            ALU.add).then_inc(done[s]["x_added"], 1)
                elif name == "project":
                    wait_filled(v, r, s, step)
                    nc.vector.scalar_tensor_tensor(out=HN[s][:, i], in0=bank_of(s, step)[:, 0:D], scalar=1.0 / WS,
                                                   in1=X[s][:, i], op0=ALU.mult, op1=ALU.add).then_inc(done[s]["y"], 1)
                    if i == G - 1:
                        wait_for(v, r, s, "y", step)
                        v.sem_inc(x_free[s], 1)
                elif name == "gram":
                    wait_filled(v, r, s, step)
                    if layer in (DIR_A, DIR_B):
                        hand_over(nc.vector.tensor_tensor(
                            U2[s].rearrange("p g w k -> p (g w k)"), bank_of(s, step)[:, :],
                            AA[s][:].rearrange("p g w k -> p (g w k)"), ALU.mult), r, s, step, 0)
                        nc.vector.tensor_tensor(UW[s], U2[s][:, :, 0], U2[s][:, :, 1], ALU.add).then_inc(done[s]["gram"], 1)
                    else:
                        u = bank_of(s, step)[:, 0:TOK].rearrange("p (g k) -> p g k", g=G)
                        hand_over(nc.vector.tensor_reduce(SE[s][:], u, AX_X, ALU.max), r, s, step, 0)
                        nc.vector.tensor_tensor(UW2[s], u, SE[s][:].unsqueeze(2).broadcast_to((P, G, P)),
                                                ALU.subtract).then_inc(done[s]["gram"], 1)
                elif name == "soft":
                    wait_for(v, r, s, "gram_exp", ("gram", layer, None))
                    if layer in (DIG_A, DIG_B):
                        nc.vector.tensor_reduce(SE[s][:], E[s], AX_X, ALU.add)
                    hand_over(nc.vector.tensor_tensor(DL[s], E[s], A[s][:], ALU.mult), r, s, step, 0)
                    hand_over(nc.vector.tensor_reduce(SD[s][:], DL[s], AX_X, ALU.add), r, s, step, 1)
                    if layer in (DIG_A, DIG_B):
                        hand_over(nc.vector.scalar_tensor_tensor(out=SD[s][:], in0=SE[s][:], scalar=1e-10, in1=SD[s][:],
                                                                 op0=ALU.mult, op1=ALU.add), r, s, step, 2)
                    else:
                        hand_over(nc.vector.tensor_scalar(SD[s][:], SD[s][:], 1e-10, None, ALU.add), r, s, step, 2)
                    hand_over(nc.vector.reciprocal(SR[s][:], SD[s][:]), r, s, step, 3)
                    nc.vector.tensor_tensor(DL[s], DL[s], SR[s][:].unsqueeze(2).broadcast_to((P, G, P)),
                                            ALU.mult).then_inc(done[s]["soft"], 1)
                elif name == "aturn" and layer in (DIG_A, DIG_B):
                    wait_filled(v, r, s, step)
                    for w in range(3):
                        last = nc.vector.tensor_tensor(
                            AT[s][:, w], bank_of(s, step)[:, 0:TOK].rearrange("p (g k) -> p g k", g=G),
                            tri_dig[:, w, :].unsqueeze(1).broadcast_to((P, G, P)), ALU.mult)
                    last.then_inc(done[s]["aturn_dig"], 1)
                elif name == "context":
                    wait_filled(v, r, s, step)
                    hand_over(nc.vector.bn_stats(ST[s][:, i], bank_of(s, step)[:, 0:D]), r, s, step, 0)
                elif name == "cstats":
                    nc.vector.memset(pad_col[:], 0.0)
                    for g in range(G):
                        last = nc.vector.bn_aggr(MV[s][:, g], ST[s][:, g])
                    hand_over(last, r, s, step, 0)
                    if layer in (DIR_A, DIR_B):
                        nc.vector.tensor_scalar(VE[s][:], MV[s][:, :, 1], D / (D - 1.0), 1e-30, ALU.mult,
                                                ALU.max).then_inc(done[s]["cvar"], 1)
                    else:
                        nc.vector.tensor_scalar(VE[s][:], MV[s][:, :, 1], 1e-12, None, ALU.add).then_inc(done[s]["cvar"], 1)
                elif name == "cshift":
                    wait_for(v, r, s, "crstd", ("cstats", layer, None))
                    over = RS[s][:]
                    if layer in (DIR_A, DIR_B):
                        hand_over(nc.vector.tensor_scalar(SR[s][:], RS[s][:], 1e-3, None, ALU.add), r, s, step, 0)
                        hand_over(nc.vector.reciprocal(RI[s][:], SR[s][:]), r, s, step, 1)
                        over = RI[s][:]
                    nc.vector.scalar_tensor_tensor(out=SH[s][:], in0=MV[s][:, :, 0], scalar=-1.0, in1=over,
                                                   op0=ALU.mult, op1=ALU.mult).then_inc(done[s]["cshift"], 1)
                elif name == "residual":
                    wait_for(v, r, s, "affine", ("affine", layer, None))
                    nc.vector.scalar_tensor_tensor(out=X[s][:], in0=HN[s][:], scalar=0.0, in1=X[s][:], op0=ALU.max,
                                                   op1=ALU.add).then_inc(done[s]["x_added"], 1)

            rounds(v, "vector", step_of)

        @block.tensor
        def _(pe):
            pe.wait_ge(consts_done, 1)
            pe.wait_ge(setup_done, 1)

            def product(out, left, right, first=True, last=True):
                n = 0
                for (lh, ll), (rh, rl) in zip(left, right):
                    for a, b in ((lh, rh), (lh, rl), (ll, rh)):
                        m = nc.tensor.matmul(out, a, b, start=(first and n == 0), stop=(last and n == 3 * len(left) - 1))
                        n += 1
                return m

            def weight(w, c, cols=slice(0, D)):
                return w_hi[:, w, c, cols], w_lo[:, w, c, cols]

            def turned(s, c, cols=slice(0, TOK)):
                return HT[s][:, 0, c, cols], HT[s][:, 1, c, cols]

            def step_of(r, s, name, layer, i):
                step = (name, layer, i)
                wait_emptied(pe, r, s, step)
                if name == "load":
                    pe.wait_ge(x_in[s], r[0] * 32 + 32)
                    for g in range(G):
                        last = nc.tensor.transpose(bank_of(s, step)[:, g * P:(g + 1) * P], A[s][:, g], ident[:])
                    last.then_inc(filled[s], 1)
                elif name == "turn":
                    if layer in (DIR_B, DIG_B):
                        wait_for(pe, r, s, "affine", ("affine", layer - 1, None))
                    else:
                        wait_for(pe, r, s, "normed", ("norm", layer, i))
                    for c in range(C):
                        last = nc.tensor.transpose(bank_of(s, step)[:, c * P:(c + 1) * P], HN[s][:, i, c * P:(c + 1) * P],
                                                   ident[:])
                    last.then_inc(filled[s], 1)
                elif name == "proj":
                    wait_for(pe, r, s, "turn_lo", ("turn", layer, G - 1))
                    for side in range(2):
                        last = product(bank_of(s, step)[:, side * TOK:(side + 1) * TOK],
                                       [weight(W0[layer] + side, c, slice(i * P, (i + 1) * P)) for c in range(C)],
                                       [turned(s, c) for c in range(C)])
                    last.then_inc(filled[s], 1)
                elif name == "vals":
                    j, g = i // G, i % G
                    wait_for(pe, r, s, "turn_lo", ("turn", layer, g))
                    w = W0[layer] + (j if layer in (DIG_A, DIG_B) else 2)
                    product(bank_of(s, step)[:, 0:D], [turned(s, c, slice(g * P, (g + 1) * P)) for c in range(C)],
                            [weight(w, c) for c in range(C)]).then_inc(filled[s], 1)
                elif name == "scores":
                    wait_for(pe, r, s, "proj_lo", ("proj", layer, C - 1))
                    cols = slice(i * P, (i + 1) * P)
                    for c in range(C):
                        for n, (a, b) in enumerate(((0, 0), (0, 1), (1, 0))):
                            for h in range(HPC):
                                rows_h = slice(HD * h, HD * (h + 1))
                                m = nc.tensor.matmul(bank_of(s, step, h)[:, c * P:(c + 1) * P], QK[s][rows_h, a, c, 0, cols],
                                                     QK[s][rows_h, b, c, 1, cols], start=(n == 0), stop=(n == 2))
                                if c == C - 1 and n == 2:
                                    m.then_inc(filled[s], 1)
                elif name == "flip":
                    g, c = i
                    wait_for(pe, r, s, "centred", ("scores", layer, g))
                    for h in range(HPC):
                        last = nc.tensor.transpose(bank_of(s, step)[:, h * P:(h + 1) * P], T[s][:, g, HPC * c + h], ident[:])
                    last.then_inc(filled[s], 1)
                elif name == "mix":
                    for c in range(C):
                        wait_for(pe, r, s, "probs", ("flip", layer, (i, c)))
                        if c == 0:
                            wait_for(pe, r, s, "vals", ("vals", layer, i))
                        for j in range(2):
                            for h in range(HPC):
                                n = HPC * c + h
                                left = V[s][:, i, HD * n:HD * (n + 1)] if j == 0 else ones[:]
                                m = nc.tensor.matmul(bank_of(s, step, j)[HD * h:HD * (h + 1), c * P:(c + 1) * P], left,
                                                     PT[s][:, n], start=True, stop=True)
                            if c == C - 1:
                                m.then_inc(filled[s], 1)
                elif name == "back":
                    wait_for(pe, r, s, "mixed", ("mix", layer, i))
                    for c in range(C):
                        last = nc.tensor.transpose(bank_of(s, step)[:, c * P:(c + 1) * P], OT[s][:, c], ident[:])
                    last.then_inc(filled[s], 1)
                elif name == "project":
                    wait_for(pe, r, s, "mixed_lo", ("halve", layer, i))
                    product(bank_of(s, step)[:, 0:D], [(OHL[s][:, 0, c], OHL[s][:, 1, c]) for c in range(C)],
                            [weight(W0[layer] + 3, c) for c in range(C)]).then_inc(filled[s], 1)
                elif name == "gram":
                    if layer in (DIR_A, DIR_B):
                        wait_for(pe, r, s, "proj_lo", ("proj", layer, C - 1))
                        for g in range(G):
                            cols = slice(g * P, (g + 1) * P)
                            last = product(bank_of(s, step)[:, g * TOK:(g + 1) * TOK].rearrange("p (w k) -> p w k", w=2),
                                           [turned(s, c, cols) for c in range(C)],
                                           [(QK[s][:, 0, c, :, cols], QK[s][:, 1, c, :, cols]) for c in range(C)])
                    else:
                        wait_for(pe, r, s, "turn_lo", ("turn", layer, G - 1))
                        for g in range(G):
                            pair = [turned(s, c, slice(g * P, (g + 1) * P)) for c in range(C)]
                            last = product(bank_of(s, step)[:, g * P:(g + 1) * P], pair, pair)
                    last.then_inc(filled[s], 1)
                elif name == "aturn":
                    wait_for(pe, r, s, "soft", ("soft", layer, None))
                    for g in range(G):
                        last = nc.tensor.transpose(bank_of(s, step)[:, g * P:(g + 1) * P], DL[s][:, g], ident[:])
                    last.then_inc(filled[s], 1)
                elif name == "context":
                    kinds = len(ROW_V[layer])
                    wait_for(pe, r, s, "aturn_dir" if layer in (DIR_A, DIR_B) else "aturn_dig", ("aturn", layer, None))
                    wait_for(pe, r, s, "vals", ("vals", layer, (kinds - 1) * G + i))
                    for j in range(kinds):
                        last = nc.tensor.matmul(bank_of(s, step)[:, 0:D], AT[s][:, j, i], (V[s], V1[s], V2[s])[j][:, i],
                                                start=(j == 0), stop=(j == kinds - 1))
                    last.then_inc(filled[s], 1)

            rounds(pe, "tensor", step_of)


_MATRICES = [("L0_gnn_Wq", None), ("L0_gnn_Wk", None), ("L0_gnn_Wv", None),
             ("L1_gnn_W_left", 0), ("L1_gnn_W_right", 0), ("L1_gnn_W_lin", 0),
             ("L1_gnn_W_left", 1), ("L1_gnn_W_right", 1), ("L1_gnn_W_lin", 1),
             ("L2_gnn_Wl", 0), ("L2_gnn_Ws", 0), ("L2_gnn_Wr", 0), ("L2_gnn_Wl", 1), ("L2_gnn_Ws", 1), ("L2_gnn_Wr", 1),
             ("L3_gnn_Wq", None), ("L3_gnn_Wk", None), ("L3_gnn_Wv", None), ("L3_gnn_Wo", None)]
_ROWS = [("L0_gnn_bv", None), ("L1_gnn_b_lin", 0), ("L1_gnn_b_lin", 1),
         ("L2_gnn_bl", 0), ("L2_gnn_bs", 0), ("L2_gnn_br", 0), ("L2_gnn_bl", 1), ("L2_gnn_bs", 1), ("L2_gnn_br", 1),
         ("L3_gnn_bv", None), ("L3_gnn_bo", None),
         ("L1_gnn_ln_a", 0), ("L1_gnn_ln_b", 0), ("L1_gnn_ln_a", 1), ("L1_gnn_ln_b", 1),
         ("L2_gnn_ln_w", 0), ("L2_gnn_ln_b", 0), ("L2_gnn_ln_w", 1), ("L2_gnn_ln_b", 1)]


def layout(inputs):
    import numpy as np

    def pick(name, at):
        a = np.asarray(inputs[name])
        return a if at is None else a[at]

    weights = np.stack([pick(n, at) if n.startswith("L0") else pick(n, at).T for n, at in _MATRICES])
    rows = np.stack([pick(n, at) for n, at in _ROWS])
    qk = np.stack([np.asarray(inputs["L0_gnn_bq"]).reshape(C, P), np.asarray(inputs["L0_gnn_bk"]).reshape(C, P)])
    return {"x": np.ascontiguousarray(inputs["x"]), "adj": np.ascontiguousarray(inputs["adj"]),
            "weights": np.ascontiguousarray(weights), "rows": np.ascontiguousarray(rows),
            "qk_bias": np.ascontiguousarray(qk.transpose(2, 0, 1)), "beta": np.asarray(inputs["L0_gnn_beta"]).reshape(1)}


def kernel(**inputs):
    import concourse.bacc as _bacc
    from concourse import mybir as _mybir
    from concourse.bass_utils import run_bass_kernel_spmd as _run

    nc = _bacc.Bacc("TRN2", target_bir_lowering=False, num_devices=1)
    arrays, args = {}, []
    for name, a in layout(inputs).items():
        arrays[f"in_{name}_dram"] = a
        args.append(nc.dram_tensor(f"in_{name}_dram", a.shape, _mybir.dt.from_np(a.dtype), kind="ExternalInput").ap())
    args.append(nc.dram_tensor("out_dram", arrays["in_x_dram"].shape, F32, kind="ExternalOutput").ap())
    graph_layers_kernel(nc, *args)
    r = _run(nc, [arrays], core_ids=[0])
    return r.results[0]["out_dram"]
```

```python
from contextlib import ExitStack

import concourse.bass as bass
from concourse import mybir

ALU = mybir.AluOpType
ACT = mybir.ActivationFunctionType
AX_X = mybir.AxisListType.X
F32 = mybir.dt.float32
F16 = mybir.dt.float16

P = 128
D = 384
C = D // P
G = 1
STREAMS = 4
TOK = G * P
H = 12
HD = D // H
HPC = P // HD
BANKS = 8
WS = 16.0

GAT, DIR_A, DIR_B, DIG_A, DIG_B, GRAPHORMER = range(6)
ATTENTION = (GAT, GRAPHORMER)
W0 = {GAT: 0, DIR_A: 3, DIR_B: 6, DIG_A: 9, DIG_B: 12, GRAPHORMER: 15}
N_W = 19
ROW_V = {GAT: [0], DIR_A: [1], DIR_B: [2], DIG_A: [3, 4, 5], DIG_B: [6, 7, 8], GRAPHORMER: [9]}
ROW_BO = 10
ROW_LN = {DIR_A: 11, DIR_B: 13, DIG_A: 15, DIG_B: 17}
N_ROWS = 19
MASKED = -9000000000000000.0


def stream_steps():
    out = []

    def add(name, layer=None, i=None):
        out.append((name, layer, i))

    add("load")
    for layer in range(6):
        if layer not in (DIR_B, DIG_B):
            for g in range(G):
                add("stats", layer, g)
            for g in range(G):
                add("norm", layer, g)
        for g in range(G):
            add("turn", layer, g)
        if layer in ATTENTION or layer in (DIR_A, DIR_B):
            for m in range(C):
                add("proj", layer, m)
        if layer in ATTENTION:
            for g in range(G):
                add("scores", layer, g)
            for g in range(G):
                add("vals", layer, g)
            end = "back" if layer == GAT else "project"
            for g in range(G):
                if layer == GRAPHORMER:
                    add("scale", layer, g)
                for c in range(C):
                    add("flip", layer, (g, c))
                if g > 0:
                    add(end, layer, g - 1)
                add("mix", layer, g)
            add(end, layer, G - 1)
        elif layer in (DIR_A, DIR_B):
            for g in range(G):
                add("vals", layer, g)
            add("gram", layer)
            add("soft", layer)
            add("aturn", layer)
        else:
            add("gram", layer)
            for j in range(3):
                for g in range(G):
                    add("vals", layer, j * G + g)
                if j == 0:
                    add("soft", layer)
            add("aturn", layer)
        if layer not in ATTENTION:
            for g in range(G):
                add("context", layer, g)
            for g in range(G):
                add("cnorm", layer, g)
                if layer in (DIR_B, DIG_B):
                    add("residual", layer, g)
    add("finish")
    return out


TURNS = {
    "tensor": ("330332133222331101221230031332302231232320131130331220020032032101110120031020323301021310113100"
               "200031231033203212211132201003010203031310220000020212101000321012313303123213222111311201023203"
               "30310312112212323212"),
    "vector": ("122212223312321033320332302232313223103223202123132013333202123323203131123033132000302303132321"
               "002013020101323310021311013130020100023121301020103031102302012003002131003101302001000121200001"
               "0220112100031012102331210132231231121112321131212103232132302311"),
    "scalar": ("333231323111013012032202132111302200202021012111000320230331210113001203031303321223122110302311"
               "303220210210002303323310222132002330031213101231"),
    "pool": "2033212132032321031030320110002131212013",
    "sync": "0123",
}
LATE = {"tensor": [48, 35, 20], "vector": [58, 35, 20], "scalar": [30, 23, 15], "pool": [9, 5, 3], "sync": [1, 1, 1]}


def banks_of(name):
    return {"load": 1, "turn": 1, "proj": 1, "vals": 1, "scores": HPC, "flip": 1, "mix": 1, "back": 1, "project": 1,
            "gram": 1, "aturn": 1, "context": 1}.get(name, 0)


def signals_of(step):
    name, layer, i = step
    directed = layer in (DIR_A, DIR_B)
    if name == "load":
        return ["handed", "sides"]
    if name == "stats":
        return ["handed"] * 2 + ["var", "rstd"]
    if name == "norm":
        return ["normed"]
    if name == "turn":
        return ["turn_hi", "turn_lo"]
    if name == "proj":
        return ["proj_hi", "proj_lo"]
    if name == "vals":
        return ["vals"]
    if name == "scores":
        return ["scored"] * HPC + ["logits"] * C + ["exped"] * C + (
            ["sums"] * C + ["sums", "sums"] if layer == GRAPHORMER else [])
    if name == "scale":
        return ["handed"] * 3 + ["recip", "scaled", "scaled", "act_scaled"]
    if name == "flip":
        return ["probs"]
    if name == "mix":
        return ["mixed_hi", "mixed_lo"] if layer == GRAPHORMER else ["recip", "mixed_hi"]
    if name == "back":
        return ["handed", "x_added"]
    if name == "project":
        return ["y"]
    if name == "gram":
        return ["handed", "gram", "gram_exp"]
    if name == "soft":
        return ["handed"] * 4 + ["soft"]
    if name == "aturn":
        return ["aturn_dir" if directed else "aturn_dig"]
    if name == "context":
        return ["handed"] * 2 + ["var", "rstd"]
    if name == "cnorm":
        return ["centred"] + (["handed"] * 2 if directed else []) + ["normed"]
    if name == "residual":
        return ["x_added"]
    if name == "finish":
        return ["y_biased"]
    return []


def has_part(engine, step):
    name, layer, i = step
    directed = layer in (DIR_A, DIR_B)
    if engine == "tensor":
        return banks_of(name) > 0
    if engine == "vector":
        return name not in ("flip", "finish") and not (name == "aturn" and directed)
    if engine == "scalar":
        return (name in ("turn", "proj", "scores", "scale", "flip", "mix", "gram", "finish")
                or name == "aturn" and directed)
    if engine == "pool":
        return name in ("stats", "context", "finish") or name == "scores" and layer == GRAPHORMER
    return name == "load"


RELEASE = {"load": "sides", "turn": "turn_lo", "proj": "proj_lo", "vals": "vals", "scores": "scored", "flip": "probs",
           "mix": "mixed_hi",
           "back": "x_added", "project": "y", "gram": "gram"}


def release_of(step, j):
    name, layer, i = step
    if name == "aturn":
        return "aturn_dir" if layer in (DIR_A, DIR_B) else "aturn_dig", step, 0
    if name == "context":
        return "centred", ("cnorm", layer, i), 0
    if name == "mix" and layer == GRAPHORMER:
        return "mixed_lo", step, 0
    return RELEASE[name], step, j if name == "scores" else 0


def turns_of(engine, steps):
    own = [x for x in steps if has_part(engine, x)]
    queues = [[(x, 0) for x in own]]
    for late in LATE[engine]:
        queues.append([(x, 1) for x in own[late:]] + [(x, 0) for x in own[:late]])
    turns = [(s, *queues[s].pop(0)) for s in map(int, TURNS[engine])]
    assert not any(queues), engine
    return turns


class Plan:

    def __init__(self):
        self.steps = stream_steps()
        self.total, self.nth = {}, {}
        self.fills = 0
        self.fill = {}
        for step in self.steps:
            for sig in signals_of(step):
                self.nth.setdefault((sig, step), []).append(self.total.get(sig, 0))
                self.total[sig] = self.total.get(sig, 0) + 1
            self.fill[step] = self.fills
            self.fills += banks_of(step[0])
        order = [(s, step, j, back) for s, step, back in turns_of("tensor", self.steps) for j in range(banks_of(step[0]))]
        self.bank, self.users = {}, {}
        for n, (s, step, j, back) in enumerate(order):
            self.bank[s, step, j] = n % BANKS
            self.users[s, step, j] = [(*order[m], ago) for ago, top in ((0, n), (1, len(order)), (2, len(order)))
                                      for m in reversed(range(top)) if m % BANKS == n % BANKS]


def graph_layers_kernel(nc, x, adj, weights, rows, qk_bias, beta, out):
    N = x.shape[0]
    ROUNDS = N // (G * STREAMS)
    plan = Plan()
    nc.disable_value_cache = True

    with ExitStack() as ctx:
        def sb(name, shape, dt=F32):
            return ctx.enter_context(nc.sbuf_tensor(name, shape, dt))

        def sem(name):
            return ctx.enter_context(nc.semaphore(name))

        w_hi = sb("w_hi", [P, N_W, C, D], F16)
        w_lo = sb("w_lo", [P, N_W, C, D], F16)
        row = sb("row", [P, N_ROWS, D])
        bias_qk = sb("bias_qk", [P, 2, C])
        beta_col = sb("beta_col", [P, 1])
        upper = sb("upper", [P, P])
        tri = sb("tri", [P, 3, P])
        ident = tri[:, 1, :]
        powers = sb("powers", [P, 2, G])
        spare = sb("spare", [P, 1])

        X = [sb(f"x{s}", [P, G, D]) for s in range(STREAMS)]
        A = [sb(f"adj{s}", [P, G, P]) for s in range(STREAMS)]
        HN = [sb(f"h{s}", [P, G, D]) for s in range(STREAMS)]
        HT = [sb(f"ht{s}", [P, 2, C, TOK], F16) for s in range(STREAMS)]
        QK = [sb(f"qk{s}", [P, 2, C, 2, TOK], F16) for s in range(STREAMS)]
        V = [sb(f"v{s}", [P, G, D]) for s in range(STREAMS)]
        T = [sb(f"t{s}", [P, G, H, P]) for s in range(STREAMS)]
        PT = [sb(f"pt{s}", [P, H, P]) for s in range(STREAMS)]
        AA = [sb(f"aa{s}", [P, G, 2, P]) for s in range(STREAMS)]
        OT = [h[:, 0].rearrange("p (c k) -> p c k", c=C) for h in HN]
        SUMS = [h[:, 0, 0:H * P // 8].rearrange("p (h k) -> p h k", h=H) for h in HN]
        OH = [[q[:, half, :, 0, :] for half in range(2)] for q in QK]
        B0 = [p[:, 0:G] for p in PT]
        PARTS = [p[:, :, 0:P // 2] for p in PT]
        few = [sb(f"few{s}", [P, G * (6 + 2 + 6 + 4 * H)]) for s in range(STREAMS)]
        at = [0]

        def columns(width):
            at.append(at[-1] + G * width)
            return [f[:, at[-2]:at[-1]].rearrange("p (g w) -> p g w", g=G) for f in few]

        ST, MV, MX, SM, RH, AM = (columns(w) for w in (6, 2, H, H, H, H))
        VE, RS, RI, SE, SD, SR = ([v[:, :, 0] for v in columns(1)] for _ in range(6))

        flat = [T[s][:].rearrange("p g h k -> p (g h k)") for s in range(STREAMS)]
        def part(first, blocks):
            return [f[:, first * TOK:(first + blocks) * TOK].rearrange("p (w g k) -> p w g k", w=blocks, g=G) for f in flat]

        V1 = [f[:, 0:G * D].rearrange("p (g d) -> p g d", g=G) for f in flat]
        V2 = [f[:, G * D:2 * G * D].rearrange("p (g d) -> p g d", g=G) for f in flat]
        U2 = [f[:, 0:2 * TOK].rearrange("p (g w k) -> p g w k", g=G, w=2) for f in flat]
        UW = [u[:, 0] for u in part(2, 1)]
        UW2 = [u[:, 0] for u in part(6, 1)]
        E = [u[:, 0] for u in part(7, 1)]
        DL = [u[:, 0] for u in part(8, 1)]
        AT = part(9, 3)

        bank = [ctx.enter_context(nc.psum_tensor(f"bank{b}", [P, 512], F32)) for b in range(BANKS)]

        done = [{name: sem(f"{name}{s}") for name in plan.total} for s in range(STREAMS)]
        filled = [sem(f"bank_filled{s}") for s in range(STREAMS)]
        x_in = [sem(f"x_in{s}") for s in range(STREAMS)]
        x_free = [sem(f"x_free{s}") for s in range(STREAMS)]
        stored = [sem(f"stored{s}") for s in range(STREAMS)]
        w_in = [sem(f"w_in{i}") for i in range(4)]
        w_hi_done, w_lo_done = sem("w_hi_done"), sem("w_lo_done")
        vector_setup = sem("vector_setup")
        rows_in, consts_done, setup_done = sem("rows_in"), sem("consts_done"), sem("setup_done")
        pool_setup = sem("pool_setup")

        x_v = x.rearrange("(n g) p d -> n p g d", g=G)
        adj_v = adj.rearrange("(n g) p k -> n p g k", g=G)
        out_v = out.rearrange("(n g) p d -> n p g d", g=G)
        w_v = weights.rearrange("w (c p) n -> w p c n", p=P)

        def count(r, total, nth):
            it, back = r
            return it * total + (nth + 1 - back * total)

        def first_round(r):
            return isinstance(r[0], int) and r[0] == r[1]

        def wait_for(eng, r, s, sig, step, n=0):
            eng.wait_ge(done[s][sig], count(r, plan.total[sig], plan.nth[sig, step][n]))

        def wait_filled(eng, r, s, step, j=0):
            eng.wait_ge(filled[s], count(r, plan.fills, plan.fill[step] + j))

        def wait_emptied(eng, r, s, step):
            it, back = r
            need = {}
            for j in range(banks_of(step[0])):
                for s2, before, k, back2, ago in plan.users[s, step, j]:
                    if isinstance(it, int) and it - ago - back2 < 0:
                        break
                    if isinstance(it, int) and it - ago - back2 >= ROUNDS:
                        continue
                    sig, giver, n = release_of(before, k)
                    latest = (-ago - back2, plan.nth[sig, giver][n])
                    need[s2, sig] = max(need.get((s2, sig), latest), latest)
                    break
            for (s2, sig), (ago, nth) in need.items():
                ago = -ago
                assert isinstance(it, int) or ago < 2
                eng.wait_ge(done[s2][sig], count((it, ago), plan.total[sig], nth))

        def bank_of(s, step, j=0):
            return bank[plan.bank[s, step, j]]

        def rounds(eng, engine, step_of):
            turns = turns_of(engine, plan.steps)
            for s, step, back in turns:
                if not back:
                    step_of((0, 0), s, *step)
            with eng.Fori(1, ROUNDS) as it:
                for s, step, back in turns:
                    step_of((it, back), s, *step)
            for s, step, back in turns:
                if back:
                    step_of((ROUNDS, 1), s, *step)

        stage = [flat[i][:, 0:C * D].rearrange("p (c n) -> p c n", c=C) for i in range(4)]
        block = ctx.enter_context(nc.Block())

        @block.sync
        def _(sp):
            sp.dma_start(row[:], rows.rearrange("(a r) d -> a r d", a=1).broadcast_to((P, N_ROWS, D))).then_inc(rows_in, 16)
            sp.dma_start(bias_qk[:], qk_bias).then_inc(rows_in, 16)
            sp.dma_start(beta_col[:], beta.rearrange("(a b) -> a b", a=1).broadcast_to((P, 1))).then_inc(rows_in, 16)
            for w in range(N_W):
                if w >= 4:
                    sp.wait_ge(w_lo_done, w - 3)
                sp.dma_start(stage[w % 4], w_v[w]).then_inc(w_in[w % 4], 16)
            def step_of(r, s, name, layer, i):
                step = (name, layer, i)
                if name == "load":
                    if not first_round(r):
                        sp.wait_ge(x_free[s], r[0])
                    n = (r[0] - r[1]) * STREAMS + s
                    sp.dma_start(X[s][:], x_v[bass.ds(n, 1)].rearrange("a p g d -> (a p) g d")).then_inc(x_in[s], 16)
                    sp.dma_start(A[s][:], adj_v[bass.ds(n, 1)].rearrange("a p g d -> (a p) g d")).then_inc(x_in[s], 16)

            rounds(sp, "sync", step_of)

        @block.gpsimd
        def _(pool):
            n = 0

            def select(view, op, base, pattern, cm):
                nonlocal n
                nc.gpsimd.memset(view, 1.0).then_inc(pool_setup, 1)
                n += 1
                pool.wait_ge(pool_setup, n)
                return nc.gpsimd.affine_select(out=view, in_=view, compare_op=op, fill=0.0, base=base,
                                               pattern=[[pattern, P]], channel_multiplier=cm)

            select(upper[:], ALU.is_ge, 0, 1, -1)
            select(tri[:, 0, :], ALU.is_ge, -1, -1, 1)
            select(tri[:, 1, :], ALU.is_equal, 0, -1, 1)
            select(tri[:, 2, :], ALU.is_ge, -1, 1, -1)
            nc.gpsimd.memset(powers[:, 0, :], -0.5)
            nc.gpsimd.memset(powers[:, 1, :], 0.5).then_inc(consts_done, 1)
            pool.wait_ge(consts_done, 1)
            pool.wait_ge(rows_in, 48)
            def step_of(r, s, name, layer, i):
                step = (name, layer, i)
                if name == "stats":
                    wait_for(pool, r, s, "var", step)
                    nc.gpsimd.tensor_tensor(RS[s][:, i:i + 1], VE[s][:, i:i + 1], powers[:, 0, 0:1],
                                            ALU.pow).then_inc(done[s]["rstd"], 1)
                elif name == "scores":
                    if i > 0:
                        wait_for(pool, r, s, "sums", ("scores", layer, i - 1), C + 1)
                    wait_for(pool, r, s, "scored", step, HPC - 1)
                    for c in range(C):
                        some = slice(HPC * c, HPC * (c + 1))
                        nc.gpsimd.tensor_tensor(PARTS[s][:, some], T[s][:, i, some, 0:P // 2], T[s][:, i, some, P // 2:P],
                                                ALU.add).then_inc(done[s]["sums"], 1)
                    wait_for(pool, r, s, "sums", step, C - 1)
                    nc.gpsimd.tensor_tensor(PARTS[s][:, :, 0:P // 4], PARTS[s][:, :, 0:P // 4], PARTS[s][:, :, P // 4:P // 2],
                                            ALU.add).then_inc(done[s]["sums"], 1)
                    wait_for(pool, r, s, "sums", step, C)
                    nc.gpsimd.tensor_tensor(SUMS[s], PARTS[s][:, :, 0:P // 8], PARTS[s][:, :, P // 8:P // 4],
                                            ALU.add).then_inc(done[s]["sums"], 1)
                elif name == "context":
                    wait_for(pool, r, s, "var", step)
                    which = 1 if layer in (DIR_A, DIR_B) else 0
                    nc.gpsimd.tensor_tensor(RS[s][:, i:i + 1], VE[s][:, i:i + 1], powers[:, which, 0:1],
                                            ALU.pow).then_inc(done[s]["rstd"], 1)
                elif name == "finish":
                    last = ("project", GRAPHORMER, G - 1)
                    wait_for(pool, r, s, "y", last)
                    nc.gpsimd.tensor_tensor(HN[s][:], HN[s][:],
                                            row[:, ROW_BO, :].unsqueeze(1).broadcast_to((P, G, D)),
                                            ALU.add).then_inc(done[s]["y_biased"], 1)

            rounds(pool, "pool", step_of)

        @block.scalar
        def _(act):
            for w in range(N_W):
                act.wait_ge(w_in[w % 4], 16 * (w // 4 + 1))
                nc.scalar.activation(w_hi[:, w], stage[w % 4], ACT.Copy, scale=WS).then_inc(w_hi_done, 1)
            act.wait_ge(setup_done, 1)
            def step_of(r, s, name, layer, i):
                step = (name, layer, i)
                if name == "turn":
                    wait_filled(act, r, s, step)
                    nc.scalar.activation(HT[s][:, 0, :, i * P:(i + 1) * P],
                                         bank_of(s, step)[:, 0:D].rearrange("p (c k) -> p c k", c=C),
                                         ACT.Relu).then_inc(done[s]["turn_hi"], 1)
                elif name == "proj":
                    wait_filled(act, r, s, step)
                    if layer == GAT:
                        for side in range(2):
                            last = nc.scalar.activation(QK[s][:, 0, i, side], bank_of(s, step)[:, side * TOK:(side + 1) * TOK],
                                                        ACT.Identity, bias=bias_qk[:, side, i:i + 1])
                    else:
                        last = nc.scalar.activation(QK[s][:, 0, i].rearrange("p a t -> p (a t)"), bank_of(s, step)[:, 0:2 * TOK], ACT.Copy)
                    last.then_inc(done[s]["proj_hi"], 1)
                elif name == "scores":
                    for c in range(C):
                        wait_for(act, r, s, "logits", step, c)
                        if layer == GRAPHORMER:
                            wait_for(act, r, s, "sums", step, c)
                        for h in range(HPC * c, HPC * (c + 1)):
                            last = nc.scalar.activation(T[s][:, i, h], T[s][:, i, h], ACT.Exp, bias=MX[s][:, i, h:h + 1],
                                                        accum_out=SM[s][:, i, h:h + 1])
                        last.then_inc(done[s]["exped"], 1)
                elif name == "scale":
                    wait_for(act, r, s, "recip", step)
                    for h in range(HPC, 2 * HPC):
                        last = nc.scalar.activation(T[s][:, i, h], T[s][:, i, h], ACT.Copy, scale=RH[s][:, i, h:h + 1])
                    last.then_inc(done[s]["act_scaled"], 1)
                elif name == "flip":
                    g, c = i
                    wait_filled(act, r, s, step)
                    nc.scalar.activation(PT[s][:, HPC * c:HPC * (c + 1)].rearrange("p h k -> p (h k)"),
                                         bank_of(s, step)[:, :], ACT.Copy).then_inc(done[s]["probs"], 1)
                elif name == "mix":
                    wait_filled(act, r, s, step)
                    src = bank_of(s, step)[:, 0:D].rearrange("p (c k) -> p c k", c=C)
                    if layer == GRAPHORMER:
                        nc.scalar.activation(OH[s][0], src, ACT.Copy).then_inc(done[s]["mixed_hi"], 1)
                    else:
                        nc.scalar.activation(OT[s], src, ACT.Copy).then_inc(done[s]["mixed_hi"], 1)
                elif name == "gram":
                    wait_for(act, r, s, "gram", step)
                    src = UW[s] if layer in (DIR_A, DIR_B) else UW2[s]
                    scale = 1.0 / (WS * D ** 0.5) if layer in (DIR_A, DIR_B) else 1.0 / D ** 0.5
                    nc.scalar.activation(E[s], src, ACT.Exp, scale=scale).then_inc(done[s]["gram_exp"], 1)
                elif name == "aturn" and layer in (DIR_A, DIR_B):
                    wait_filled(act, r, s, step)
                    nc.scalar.activation(AT[s][:, 0].rearrange("p g k -> p (g k)"), bank_of(s, step)[:, 0:TOK],
                                         ACT.Copy).then_inc(done[s]["aturn_dir"], 1)
                elif name == "finish":
                    wait_for(act, r, s, "y_biased", step)
                    n = (r[0] - r[1]) * STREAMS + s
                    act.dma_start(out_v[bass.ds(n, 1)].rearrange("a p g d -> (a p) g d"), HN[s][:]).then_inc(stored[s], 16)

            rounds(act, "scalar", step_of)
            for s in range(STREAMS):
                act.wait_ge(stored[s], 16 * ROUNDS)

        @block.vector
        def _(v):
            def hand_over(instruction, r, s, step, n):
                instruction.then_inc(done[s]["handed"], 1)
                wait_for(v, r, s, "handed", step, n)

            v.wait_ge(rows_in, 48)
            nc.vector.tensor_scalar(bias_qk[:], bias_qk[:], WS, None, ALU.mult).then_inc(vector_setup, 1)
            for w in range(N_W):
                v.wait_ge(w_hi_done, w + 1)
                nc.vector.scalar_tensor_tensor(out=w_lo[:, w], in0=stage[w % 4], scalar=WS, in1=w_hi[:, w],
                                               op0=ALU.mult, op1=ALU.subtract).then_inc(w_lo_done, 1)
            v.wait_ge(w_lo_done, N_W)
            v.wait_ge(vector_setup, 1)
            v.wait_ge(consts_done, 1)
            v.sem_inc(setup_done, 1)

            def low_half(out, src, hi):
                return nc.vector.tensor_tensor(out, src, hi, ALU.subtract)

            def step_of(r, s, name, layer, i):
                step = (name, layer, i)
                if name == "load":
                    v.wait_ge(x_in[s], r[0] * 32 + 32)
                    a = A[s][:]
                    hand_over(nc.vector.tensor_scalar(B0[s], a, 0.0, MASKED, ALU.is_le, ALU.mult), r, s, step, 0)
                    nc.vector.scalar_tensor_tensor(out=B0[s], in0=a, scalar=beta_col[:, 0:1], in1=B0[s],
                                                   op0=ALU.mult, op1=ALU.add)
                    nc.vector.tensor_tensor(AA[s][:, :, 0, :], a, upper[:].unsqueeze(1).broadcast_to((P, G, P)),
                                            ALU.mult)
                    wait_filled(v, r, s, step)
                    nc.vector.tensor_tensor(
                        AA[s][:, :, 1, :], bank_of(s, step)[:, 0:TOK].rearrange("p (g k) -> p g k", g=G),
                        tri[:, 0, :].unsqueeze(1).broadcast_to((P, G, P)), ALU.mult).then_inc(done[s]["sides"], 1)
                elif name == "stats":
                    if layer != GAT:
                        last = {DIR_A: ("back", GAT, i), DIG_A: ("residual", DIR_B, i),
                                GRAPHORMER: ("residual", DIG_B, i)}[layer]
                        wait_for(v, r, s, "x_added", last)
                    hand_over(nc.vector.bn_stats(ST[s][:, i], X[s][:, i]), r, s, step, 0)
                    nc.vector.memset(spare[:], 0.0)
                    hand_over(nc.vector.bn_aggr(MV[s][:, i], ST[s][:, i]), r, s, step, 1)
                    nc.vector.tensor_scalar(VE[s][:, i:i + 1], MV[s][:, i, 1:2], 1e-5, None,
                                            ALU.add).then_inc(done[s]["var"], 1)
                elif name == "norm":
                    wait_for(v, r, s, "rstd", ("stats", layer, i))
                    if layer == GAT and i == 0 and not first_round(r):
                        v.wait_ge(stored[s], r[0] * 16)
                    nc.vector.tensor_scalar(HN[s][:, i], X[s][:, i], MV[s][:, i, 0:1], RS[s][:, i:i + 1], ALU.subtract,
                                            ALU.mult).then_inc(done[s]["normed"], 1)
                elif name == "turn":
                    wait_for(v, r, s, "turn_hi", step)
                    nc.vector.scalar_tensor_tensor(
                        out=HT[s][:, 1, :, i * P:(i + 1) * P], in0=bank_of(s, step)[:, 0:D].rearrange("p (c k) -> p c k", c=C),
                        scalar=0.0, in1=HT[s][:, 0, :, i * P:(i + 1) * P], op0=ALU.max,
                        op1=ALU.subtract).then_inc(done[s]["turn_lo"], 1)
                elif name == "proj":
                    wait_for(v, r, s, "proj_hi", step)
                    if layer == GAT:
                        for side in range(2):
                            last = nc.vector.scalar_tensor_tensor(
                                out=QK[s][:, 1, i, side], in0=bank_of(s, step)[:, side * TOK:(side + 1) * TOK],
                                scalar=bias_qk[:, side, i:i + 1], in1=QK[s][:, 0, i, side], op0=ALU.add, op1=ALU.subtract)
                    else:
                        last = low_half(QK[s][:, 1, i].rearrange("p a t -> p (a t)"), bank_of(s, step)[:, 0:2 * TOK],
                                        QK[s][:, 0, i].rearrange("p a t -> p (a t)"))
                    last.then_inc(done[s]["proj_lo"], 1)
                elif name == "vals":
                    wait_filled(v, r, s, step)
                    j, g = i // G, i % G
                    dst = (V[s], V1[s], V2[s])[j]
                    nc.vector.scalar_tensor_tensor(out=dst[:, g], in0=bank_of(s, step)[:, 0:D], scalar=1.0 / WS,
                                                   in1=row[:, ROW_V[layer][j], :], op0=ALU.mult,
                                                   op1=ALU.add).then_inc(done[s]["vals"], 1)
                elif name == "scores":
                    edge = B0[s] if layer == GAT else A[s]
                    scale = (1.0 / HD ** 0.5 if layer == GAT else 1.0 / D ** 0.5) / (WS * WS)
                    heads = T[s][:, i].rearrange("p (c h) k -> p c h k", h=HPC)
                    for h in range(HPC):
                        wait_filled(v, r, s, step, h)
                        nc.vector.scalar_tensor_tensor(
                            out=heads[:, :, h, :], in0=bank_of(s, step, h)[:, 0:D].rearrange("p (c k) -> p c k", c=C),
                            scalar=scale, in1=edge[:, i, :].unsqueeze(1).broadcast_to((P, C, P)), op0=ALU.mult,
                            op1=ALU.add).then_inc(done[s]["scored"], 1)
                    wait_for(v, r, s, "scored", step, HPC - 1)
                    for c in range(C):
                        some = slice(HPC * c, HPC * (c + 1))
                        nc.vector.tensor_reduce(MX[s][:, i, some], T[s][:, i, some], AX_X, ALU.max,
                                                negate=True).then_inc(done[s]["logits"], 1)
                elif name == "scale":
                    wait_for(v, r, s, "sums", ("scores", layer, i), C + 1)
                    hand_over(nc.vector.tensor_reduce(AM[s][:, i], SUMS[s], AX_X, ALU.add), r, s, step, 0)
                    hand_over(nc.vector.tensor_tensor(AM[s][:, i], AM[s][:, i], MX[s][:, i], ALU.min), r, s, step, 1)
                    wait_for(v, r, s, "exped", ("scores", layer, i), C - 1)
                    hand_over(nc.vector.reciprocal(RH[s][:, i], SM[s][:, i]), r, s, step, 2)
                    nc.vector.scalar_tensor_tensor(out=RH[s][:, i], in0=AM[s][:, i], scalar=0.0, in1=RH[s][:, i],
                                                   op0=ALU.is_lt, op1=ALU.mult).then_inc(done[s]["recip"], 1)
                    wait_for(v, r, s, "recip", step)
                    for c in (0, C - 1):
                        some = slice(HPC * c, HPC * (c + 1))
                        nc.vector.tensor_tensor(T[s][:, i, some], T[s][:, i, some],
                                                RH[s][:, i, some].unsqueeze(2).broadcast_to((P, HPC, P)),
                                                ALU.mult).then_inc(done[s]["scaled"], 1)
                elif name == "mix":
                    if layer == GAT:
                        wait_for(v, r, s, "exped", ("scores", layer, i), C - 1)
                        nc.vector.reciprocal(RH[s][:, i], SM[s][:, i]).then_inc(done[s]["recip"], 1)
                    else:
                        wait_for(v, r, s, "mixed_hi", step)
                        low_half(OH[s][1], bank_of(s, step)[:, 0:D].rearrange("p (c k) -> p c k", c=C),
                                 OH[s][0]).then_inc(done[s]["mixed_lo"], 1)
                elif name == "back":
                    wait_filled(v, r, s, step)
                    wait_for(v, r, s, "recip", ("mix", layer, i))
                    hand_over(nc.vector.tensor_tensor(
                        flat[s][:, 0:D].rearrange("p (h k) -> p h k", h=H), bank_of(s, step)[:, 0:D].rearrange("p (h k) -> p h k", h=H),
                        RH[s][:, i].unsqueeze(2).broadcast_to((P, H, HD)), ALU.mult), r, s, step, 0)
                    nc.vector.tensor_tensor(X[s][:, i], flat[s][:, 0:D], X[s][:, i], ALU.add).then_inc(done[s]["x_added"], 1)
                elif name == "project":
                    wait_filled(v, r, s, step)
                    nc.vector.scalar_tensor_tensor(out=HN[s][:, i], in0=bank_of(s, step)[:, 0:D], scalar=1.0 / WS,
                                                   in1=X[s][:, i], op0=ALU.mult, op1=ALU.add).then_inc(done[s]["y"], 1)
                    if i == G - 1:
                        wait_for(v, r, s, "y", step)
                        v.sem_inc(x_free[s], 1)
                elif name == "gram":
                    wait_filled(v, r, s, step)
                    if layer in (DIR_A, DIR_B):
                        hand_over(nc.vector.tensor_tensor(
                            U2[s].rearrange("p g w k -> p (g w k)"), bank_of(s, step)[:, 0:2 * TOK],
                            AA[s][:].rearrange("p g w k -> p (g w k)"), ALU.mult), r, s, step, 0)
                        nc.vector.tensor_tensor(UW[s], U2[s][:, :, 0], U2[s][:, :, 1], ALU.add).then_inc(done[s]["gram"], 1)
                    else:
                        u = bank_of(s, step)[:, 0:TOK].rearrange("p (g k) -> p g k", g=G)
                        hand_over(nc.vector.tensor_reduce(SE[s], u, AX_X, ALU.max), r, s, step, 0)
                        nc.vector.tensor_tensor(UW2[s], u, SE[s].unsqueeze(2).broadcast_to((P, G, P)),
                                                ALU.subtract).then_inc(done[s]["gram"], 1)
                elif name == "soft":
                    wait_for(v, r, s, "gram_exp", ("gram", layer, None))
                    if layer in (DIG_A, DIG_B):
                        nc.vector.tensor_reduce(SE[s], E[s], AX_X, ALU.add)
                    hand_over(nc.vector.tensor_tensor(DL[s], E[s], A[s][:], ALU.mult), r, s, step, 0)
                    hand_over(nc.vector.tensor_reduce(SD[s], DL[s], AX_X, ALU.add), r, s, step, 1)
                    if layer in (DIG_A, DIG_B):
                        hand_over(nc.vector.scalar_tensor_tensor(out=SD[s], in0=SE[s], scalar=1e-10, in1=SD[s],
                                                                 op0=ALU.mult, op1=ALU.add), r, s, step, 2)
                    else:
                        hand_over(nc.vector.tensor_scalar(SD[s], SD[s], 1e-10, None, ALU.add), r, s, step, 2)
                    hand_over(nc.vector.reciprocal(SR[s], SD[s]), r, s, step, 3)
                    nc.vector.tensor_tensor(DL[s], DL[s], SR[s].unsqueeze(2).broadcast_to((P, G, P)),
                                            ALU.mult).then_inc(done[s]["soft"], 1)
                elif name == "aturn" and layer in (DIG_A, DIG_B):
                    wait_filled(v, r, s, step)
                    for w in range(3):
                        last = nc.vector.tensor_tensor(
                            AT[s][:, w], bank_of(s, step)[:, 0:TOK].rearrange("p (g k) -> p g k", g=G),
                            tri[:, w, :].unsqueeze(1).broadcast_to((P, G, P)), ALU.mult)
                    last.then_inc(done[s]["aturn_dig"], 1)
                elif name == "context":
                    wait_filled(v, r, s, step)
                    hand_over(nc.vector.bn_stats(ST[s][:, i], bank_of(s, step)[:, 0:D]), r, s, step, 0)
                    nc.vector.memset(spare[:], 0.0)
                    hand_over(nc.vector.bn_aggr(MV[s][:, i], ST[s][:, i]), r, s, step, 1)
                    if layer in (DIR_A, DIR_B):
                        last = nc.vector.tensor_scalar(VE[s][:, i:i + 1], MV[s][:, i, 1:2], D / (D - 1.0), 1e-30, ALU.mult,
                                                       ALU.max)
                    else:
                        last = nc.vector.tensor_scalar(VE[s][:, i:i + 1], MV[s][:, i, 1:2], 1e-12, None, ALU.add)
                    last.then_inc(done[s]["var"], 1)
                elif name == "cnorm":
                    at = ROW_LN[layer]
                    nc.vector.scalar_tensor_tensor(
                        out=HN[s][:, i], in0=bank_of(s, ("context", layer, i))[:, 0:D], scalar=MV[s][:, i, 0:1],
                        in1=row[:, at, :], op0=ALU.subtract, op1=ALU.mult).then_inc(done[s]["centred"], 1)
                    wait_for(v, r, s, "rstd", ("context", layer, i))
                    over = RS[s]
                    if layer in (DIR_A, DIR_B):
                        hand_over(nc.vector.tensor_scalar(SR[s][:, i:i + 1], RS[s][:, i:i + 1], 1e-3, None, ALU.add),
                                  r, s, step, 0)
                        hand_over(nc.vector.reciprocal(RI[s][:, i:i + 1], SR[s][:, i:i + 1]), r, s, step, 1)
                        over = RI[s]
                    wait_for(v, r, s, "centred", step)
                    nc.vector.scalar_tensor_tensor(out=HN[s][:, i], in0=HN[s][:, i], scalar=over[:, i:i + 1],
                                                   in1=row[:, at + 1, :], op0=ALU.mult,
                                                   op1=ALU.add).then_inc(done[s]["normed"], 1)
                elif name == "residual":
                    wait_for(v, r, s, "normed", ("cnorm", layer, i))
                    nc.vector.scalar_tensor_tensor(out=X[s][:, i], in0=HN[s][:, i], scalar=0.0, in1=X[s][:, i], op0=ALU.max,
                                                   op1=ALU.add).then_inc(done[s]["x_added"], 1)

            rounds(v, "vector", step_of)

        @block.tensor
        def _(pe):
            pe.wait_ge(consts_done, 1)
            pe.wait_ge(setup_done, 1)

            def product(out, left, right, first=True, last=True):
                n = 0
                for (lh, ll), (rh, rl) in zip(left, right):
                    for a, b in ((lh, rh), (lh, rl), (ll, rh)):
                        m = nc.tensor.matmul(out, a, b, start=(first and n == 0), stop=(last and n == 3 * len(left) - 1))
                        n += 1
                return m

            def weight(w, c, cols=slice(0, D)):
                return w_hi[:, w, c, cols], w_lo[:, w, c, cols]

            def turned(s, c, cols=slice(0, TOK)):
                return HT[s][:, 0, c, cols], HT[s][:, 1, c, cols]

            def step_of(r, s, name, layer, i):
                step = (name, layer, i)
                wait_emptied(pe, r, s, step)
                if name == "load":
                    pe.wait_ge(x_in[s], r[0] * 32 + 32)
                    for g in range(G):
                        last = nc.tensor.transpose(bank_of(s, step)[:, g * P:(g + 1) * P], A[s][:, g], ident)
                    last.then_inc(filled[s], 1)
                elif name == "turn":
                    if layer in (DIR_B, DIG_B):
                        wait_for(pe, r, s, "normed", ("cnorm", layer - 1, i))
                    else:
                        wait_for(pe, r, s, "normed", ("norm", layer, i))
                    for c in range(C):
                        last = nc.tensor.transpose(bank_of(s, step)[:, c * P:(c + 1) * P], HN[s][:, i, c * P:(c + 1) * P],
                                                   ident)
                    last.then_inc(filled[s], 1)
                elif name == "proj":
                    wait_for(pe, r, s, "turn_lo", ("turn", layer, G - 1))
                    for side in range(2):
                        last = product(bank_of(s, step)[:, side * TOK:(side + 1) * TOK],
                                       [weight(W0[layer] + side, c, slice(i * P, (i + 1) * P)) for c in range(C)],
                                       [turned(s, c) for c in range(C)])
                    last.then_inc(filled[s], 1)
                elif name == "vals":
                    j, g = i // G, i % G
                    wait_for(pe, r, s, "turn_lo", ("turn", layer, g))
                    w = W0[layer] + (j if layer in (DIG_A, DIG_B) else 2)
                    product(bank_of(s, step)[:, 0:D], [turned(s, c, slice(g * P, (g + 1) * P)) for c in range(C)],
                            [weight(w, c) for c in range(C)]).then_inc(filled[s], 1)
                elif name == "scores":
                    wait_for(pe, r, s, "proj_lo", ("proj", layer, C - 1))
                    cols = slice(i * P, (i + 1) * P)
                    for c in range(C):
                        for n, (a, b) in enumerate(((0, 0), (0, 1), (1, 0))):
                            for h in range(HPC):
                                rows_h = slice(HD * h, HD * (h + 1))
                                m = nc.tensor.matmul(bank_of(s, step, h)[:, c * P:(c + 1) * P], QK[s][rows_h, a, c, 0, cols],
                                                     QK[s][rows_h, b, c, 1, cols], start=(n == 0), stop=(n == 2))
                                if c == C - 1 and n == 2:
                                    m.then_inc(filled[s], 1)
                elif name == "flip":
                    g, c = i
                    if layer == GAT:
                        wait_for(pe, r, s, "exped", ("scores", layer, g), c)
                    else:
                        wait_for(pe, r, s, ("scaled", "act_scaled", "scaled")[c], ("scale", layer, g), (0, 0, 1)[c])
                    for h in range(HPC):
                        last = nc.tensor.transpose(bank_of(s, step)[:, h * P:(h + 1) * P], T[s][:, g, HPC * c + h], ident)
                    last.then_inc(filled[s], 1)
                elif name == "mix":
                    for c in range(C):
                        wait_for(pe, r, s, "probs", ("flip", layer, (i, c)))
                        if c == 0:
                            wait_for(pe, r, s, "vals", ("vals", layer, i))
                        for h in range(HPC):
                            n = HPC * c + h
                            m = nc.tensor.matmul(bank_of(s, step)[HD * h:HD * (h + 1), c * P:(c + 1) * P],
                                                 V[s][:, i, HD * n:HD * (n + 1)], PT[s][:, n], start=True, stop=True)
                    m.then_inc(filled[s], 1)
                elif name == "back":
                    wait_for(pe, r, s, "mixed_hi", ("mix", layer, i))
                    for c in range(C):
                        last = nc.tensor.transpose(bank_of(s, step)[:, c * P:(c + 1) * P], OT[s][:, c], ident)
                    last.then_inc(filled[s], 1)
                elif name == "project":
                    wait_for(pe, r, s, "mixed_lo", ("mix", layer, i))
                    product(bank_of(s, step)[:, 0:D], [(OH[s][0][:, c], OH[s][1][:, c]) for c in range(C)],
                            [weight(W0[layer] + 3, c) for c in range(C)]).then_inc(filled[s], 1)
                elif name == "gram":
                    if layer in (DIR_A, DIR_B):
                        wait_for(pe, r, s, "proj_lo", ("proj", layer, C - 1))
                        for g in range(G):
                            cols = slice(g * P, (g + 1) * P)
                            last = product(bank_of(s, step)[:, g * 2 * P:(g + 1) * 2 * P].rearrange("p (w k) -> p w k", w=2),
                                           [turned(s, c, cols) for c in range(C)],
                                           [(QK[s][:, 0, c, :, cols], QK[s][:, 1, c, :, cols]) for c in range(C)])
                    else:
                        wait_for(pe, r, s, "turn_lo", ("turn", layer, G - 1))
                        for g in range(G):
                            pair = [turned(s, c, slice(g * P, (g + 1) * P)) for c in range(C)]
                            last = product(bank_of(s, step)[:, g * P:(g + 1) * P], pair, pair)
                    last.then_inc(filled[s], 1)
                elif name == "aturn":
                    wait_for(pe, r, s, "soft", ("soft", layer, None))
                    for g in range(G):
                        last = nc.tensor.transpose(bank_of(s, step)[:, g * P:(g + 1) * P], DL[s][:, g], ident)
                    last.then_inc(filled[s], 1)
                elif name == "context":
                    kinds = len(ROW_V[layer])
                    wait_for(pe, r, s, "aturn_dir" if layer in (DIR_A, DIR_B) else "aturn_dig", ("aturn", layer, None))
                    wait_for(pe, r, s, "vals", ("vals", layer, (kinds - 1) * G + i))
                    for j in range(kinds):
                        last = nc.tensor.matmul(bank_of(s, step)[:, 0:D], AT[s][:, j, i], (V[s], V1[s], V2[s])[j][:, i],
                                                start=(j == 0), stop=(j == kinds - 1))
                    last.then_inc(filled[s], 1)

            rounds(pe, "tensor", step_of)


_MATRICES = [("L0_gnn_Wq", None), ("L0_gnn_Wk", None), ("L0_gnn_Wv", None),
             ("L1_gnn_W_left", 0), ("L1_gnn_W_right", 0), ("L1_gnn_W_lin", 0),
             ("L1_gnn_W_left", 1), ("L1_gnn_W_right", 1), ("L1_gnn_W_lin", 1),
             ("L2_gnn_Wl", 0), ("L2_gnn_Ws", 0), ("L2_gnn_Wr", 0), ("L2_gnn_Wl", 1), ("L2_gnn_Ws", 1), ("L2_gnn_Wr", 1),
             ("L3_gnn_Wq", None), ("L3_gnn_Wk", None), ("L3_gnn_Wv", None), ("L3_gnn_Wo", None)]
_ROWS = [("L0_gnn_bv", None), ("L1_gnn_b_lin", 0), ("L1_gnn_b_lin", 1),
         ("L2_gnn_bl", 0), ("L2_gnn_bs", 0), ("L2_gnn_br", 0), ("L2_gnn_bl", 1), ("L2_gnn_bs", 1), ("L2_gnn_br", 1),
         ("L3_gnn_bv", None), ("L3_gnn_bo", None),
         ("L1_gnn_ln_a", 0), ("L1_gnn_ln_b", 0), ("L1_gnn_ln_a", 1), ("L1_gnn_ln_b", 1),
         ("L2_gnn_ln_w", 0), ("L2_gnn_ln_b", 0), ("L2_gnn_ln_w", 1), ("L2_gnn_ln_b", 1)]


def layout(inputs):
    import numpy as np

    def pick(name, at):
        a = np.asarray(inputs[name])
        return a if at is None else a[at]

    weights = np.stack([pick(n, at) if n.startswith("L0") else pick(n, at).T for n, at in _MATRICES])
    rows = np.stack([pick(n, at) for n, at in _ROWS])
    qk = np.stack([np.asarray(inputs["L0_gnn_bq"]).reshape(C, P), np.asarray(inputs["L0_gnn_bk"]).reshape(C, P)])
    return {"x": np.ascontiguousarray(inputs["x"]), "adj": np.ascontiguousarray(inputs["adj"]),
            "weights": np.ascontiguousarray(weights), "rows": np.ascontiguousarray(rows),
            "qk_bias": np.ascontiguousarray(qk.transpose(2, 0, 1)), "beta": np.asarray(inputs["L0_gnn_beta"]).reshape(1)}


def kernel(**inputs):
    import concourse.bacc as _bacc
    from concourse import mybir as _mybir
    from concourse.bass_utils import run_bass_kernel_spmd as _run

    nc = _bacc.Bacc("TRN2", target_bir_lowering=False, num_devices=1)
    arrays, args = {}, []
    for name, a in layout(inputs).items():
        arrays[f"in_{name}_dram"] = a
        args.append(nc.dram_tensor(f"in_{name}_dram", a.shape, _mybir.dt.from_np(a.dtype), kind="ExternalInput").ap())
    args.append(nc.dram_tensor("out_dram", arrays["in_x_dram"].shape, F32, kind="ExternalOutput").ap())
    graph_layers_kernel(nc, *args)
    r = _run(nc, [arrays], core_ids=[0])
    return r.results[0]["out_dram"]
```
